# Optimizing a Trainium2 kernel written in Bass

```python
import numpy as np
import jax
import jax.numpy as jnp

def _softmax(x, axis=-1):
    return jax.nn.softmax(x, axis=axis)

def _gelu(x):
    return jax.nn.gelu(x, approximate=True)

def _silu(x):
    return jax.nn.silu(x)

def _sigmoid(x):
    return jax.nn.sigmoid(x)

def _layernorm(x, axis=-1, eps=1e-05):
    m = jnp.mean(x, axis=axis, keepdims=True)
    v = jnp.var(x, axis=axis, keepdims=True)
    return (x - m) / jnp.sqrt(v + eps)

def _scatter_add(tgt, idx, src, axis=0):
    return tgt.at[idx].add(src)

def _segment_sum(src, seg, n):
    return jax.ops.segment_sum(src, seg, n)
kernel_name = 'mk_adj_resnorm_d1_adj_r2_39b7d7'

def setup_inputs(seed: int=0):
    np.random.seed(seed)
    _w = jnp.asarray

    def _rec_inputs():
        import jax
        import jax.numpy as jnp
        _gk = jax.random.key(seed)
        x = -0.001547 + 1.001 * jax.random.normal(jax.random.fold_in(_gk, 1), (64, 128, 128), jnp.float32)
        _a = jax.random.bernoulli(jax.random.fold_in(_gk, 2), 0.03125, (64, 128, 128))
        _a = jnp.logical_or(_a, jnp.swapaxes(_a, -1, -2))
        _a = jnp.logical_or(_a, jnp.eye(128, dtype=bool))
        _af = _a.astype(jnp.float32)
        _af = _af * jax.random.uniform(jax.random.fold_in(_gk, 3), (64, 128, 128), jnp.float32, 0.05, 0.999994)
        adj = _af
        return (x, adj)
    x, adj = _rec_inputs()

    def _L0_gnn_setup():
        import jax, jax.numpy as jnp
        import numpy as np
        B, N, D, L = (4, 256, 128, 2)
        key = jax.random.key(seed)
        ks = jax.random.split(key, 6)
        node_feats = jax.random.normal(ks[0], (B, N, D), dtype=jnp.float32)
        adj_mask = jax.random.uniform(ks[1], (B, N, N), dtype=jnp.float32)
        w1 = jax.random.normal(ks[2], (L, D, 2 * D), dtype=jnp.float32) * 0.05
        b1 = jax.random.normal(ks[3], (L, D), dtype=jnp.float32) * 0.05
        w2 = jax.random.normal(ks[4], (L, D, D), dtype=jnp.float32) * 0.05
        b2 = jax.random.normal(ks[5], (L, D), dtype=jnp.float32) * 0.05
        return {'node_feats': node_feats, 'adj_mask': adj_mask, 'w1': w1, 'b1': b1, 'w2': w2, 'b2': b2}
    _L0_gnn_all = _L0_gnn_setup()
    _L0_gnn_in = {k: v for k, v in _L0_gnn_all.items() if k in ('w1', 'b1', 'w2', 'b2')}
    del _L0_gnn_all
    return {'x': x, 'adj': adj, 'L0_gnn_w1': _L0_gnn_in['w1'], 'L0_gnn_b1': _L0_gnn_in['b1'], 'L0_gnn_w2': _L0_gnn_in['w2'], 'L0_gnn_b2': _L0_gnn_in['b2']}

def reference(x, adj, L0_gnn_w1, L0_gnn_b1, L0_gnn_w2, L0_gnn_b2):
    import jax
    import jax.numpy as jnp

    def _L0_gnn_ref(node_feats, adj_mask, w1, b1, w2, b2):
        import jax, jax.numpy as jnp
        import numpy as np
        B, N, D, L = (4, 256, 128, 2)
        h = node_feats
        d = h.shape[-1]
        n_layers = w1.shape[0]
        for l in range(n_layers):
            wi = w1[l][:, :d]
            wj = w1[l][:, d:]
            ai = jnp.einsum('bnd,od->bno', h, wi)
            aj = jnp.einsum('bnd,od->bno', h, wj)
            m = jax.nn.relu(ai[:, :, None, :] + aj[:, None, :, :] + b1[l])
            m = jnp.einsum('bijd,od->bijo', m, w2[l]) + b2[l]
            m = m * adj_mask[..., None]
            msg = m.sum(axis=2)
            h = h + msg
        return h
    x = _layernorm(x + _L0_gnn_ref(x, adj, L0_gnn_w1, L0_gnn_b1, L0_gnn_w2, L0_gnn_b2), axis=-1)
    return x

_drawn_inputs = setup_inputs


def setup_inputs(seed=0):
    import zlib

    import numpy as np

    out = dict(_drawn_inputs(seed))
    spreads = {}
    factors = {}
    for name, (base, spread) in spreads.items():
        noise = np.random.default_rng([zlib.crc32(name.encode()), seed]).standard_normal(out[name].shape)
        drawn = base * np.exp(spread * noise) if base else spread * noise
        out[name] = jnp.asarray(drawn.astype(out[name].dtype))
    for name, factor in factors.items():
        out[name] = (out[name] * factor).astype(out[name].dtype)
    return out
```

```python
import numpy as np
import concourse.bass as bass
from concourse import mybir
from contextlib import ExitStack


NODES = 128
D = 128
GRAPHS = 64
LAYERS = 2
GROUP = 4
GROUPS = GRAPHS // GROUP
EPS = 1e-5

REGIONS = [(2, 26), (6, 18), (8, 15), (8, 14), (8, 13), (16, 12), (16, 11), (16, 10), (16, 9), (16, 8), (16, 7)]
SLOTS = sum(r * c for r, c in REGIONS)
TILES = SLOTS // 128
QUADS = -(-TILES // 4)
BLOCKS = NODES // 32
SLOTS_PER_GROUP = 2 * GROUP
UNITS = SLOTS_PER_GROUP * QUADS
assert sum(r for r, _ in REGIONS) == NODES and SLOTS % 128 == 0


def slot_rows():
    rows, ranks, r0 = [], [], 0
    for n, cap in REGIONS:
        for k in range(cap):
            for i in range(n):
                rows.append(r0 + i)
                ranks.append(k)
        r0 += n
    return np.array(rows), np.array(ranks)


ROWS, RANKS = slot_rows()
WINDOWS = [(int(ROWS[128 * t:128 * t + 128].min()), int(ROWS[128 * t:128 * t + 128].max()) + 1) for t in range(TILES)]
WOFF = [sum(hi - lo for lo, hi in WINDOWS[:t]) for t in range(TILES + 1)]
PAIRS = [(t, b) for t in range(TILES) for b in range(WINDOWS[t][0] // 32, (WINDOWS[t][1] - 1) // 32 + 1)]


def constants():
    def bits(a):
        return (np.ascontiguousarray(a, np.float32).view(np.uint32) >> 16).astype(np.uint16)
    p = np.arange(128)
    caps = np.zeros(128)
    np.maximum.at(caps, ROWS, RANKS + 1)
    mask = np.zeros((128, WOFF[-1]))
    for t, (lo, hi) in enumerate(WINDOWS):
        mask[p, WOFF[t] + ROWS[128 * t:128 * t + 128] - lo] = 1
    pick = np.zeros((128, len(PAIRS), 128))
    for n, (t, b) in enumerate(PAIRS):
        for e in range(128):
            r = ROWS[128 * t + e] - 32 * b
            if 0 <= r < 32:
                pick[3 * r:3 * r + 3, n, e] = 1
    tie = (127 - p) / 128
    f = [np.eye(128), np.broadcast_to(p, (128, 128)), np.broadcast_to(caps, (128, 128)), tie[:, None], mask]
    b = [np.eye(128), np.triu(np.ones((128, 128))), np.ones((128, 128)), np.tile(np.diag(tie), (1, GROUP)),
         np.broadcast_to(RANKS + 1, (128, SLOTS)), pick.reshape(128, -1)]
    return (np.concatenate([np.asarray(a, np.float32) for a in f], 1),
            np.concatenate([bits(a) for a in b], 1))


def gnn_kernel(nc, x, adj, w1, b1, w2, b2, cf, cb, out):
    f32, bf16, u16 = mybir.dt.float32, mybir.dt.bfloat16, mybir.dt.uint16
    ALU, ACT, AX = mybir.AluOpType, mybir.ActivationFunctionType, mybir.AxisListType
    ctx = ExitStack()
    with ctx:
        def sb(name, shape, dt=f32):
            return ctx.enter_context(nc.sbuf_tensor(name, shape, dt))

        def sem(name):
            return ctx.enter_context(nc.semaphore(name))

        CF = sb("CF", [128, cf.shape[1]])
        CB = sb("CB", [128, cb.shape[1]], bf16)
        ident, iota, caps, tie = CF[:, 0:128], CF[:, 128:256], CF[:, 256:384], CF[:, 384:385]
        mask = CF[:, 385:385 + WOFF[-1]]
        identb, upto, onesb, tiediag = CB[:, 0:128], CB[:, 128:256], CB[:, 256:384], CB[:, 384:384 + 512]
        rankc = CB[:, 896:896 + SLOTS]
        pick = CB[:, 896 + SLOTS:].rearrange("p (n e) -> p n e", e=128)
        w1_in = sb("w1_in", [128, LAYERS, 2 * D])
        w2_in = sb("w2_in", [128, LAYERS, D])
        w1T = sb("w1T", [128, LAYERS, 2 * D])
        w2T = sb("w2T", [128, LAYERS, D])
        b1row = sb("b1row", [128, LAYERS, D])
        b2col = sb("b2col", [128, LAYERS])

        adj_in = sb("adj_in", [128, GROUP, NODES])
        x_in = sb("x_in", [128, GROUP, D])
        junk = sb("junk", [128, GROUP, 128], bf16)
        deg = sb("deg", [128, GROUP])
        key = sb("key", [128, GROUP])
        degdiag = sb("degdiag", [128, GROUP, 128], bf16)
        above = sb("above", [128, GROUP, 128], bf16)
        place = sb("place", [128, GROUP])
        perm = sb("perm", [128, GROUP, 128])
        permT = sb("permT", [128, GROUP, 128])
        adj1 = sb("adj1", [128, GROUP, 128])
        adj2 = sb("adj2", [128, GROUP, 128])
        adjrest = sb("adjrest", [128, GROUP, 128])
        adjp = sb("adjp", [128, 3, GROUP, 128], bf16)
        nz = sb("nz", [128, GROUP, 128], bf16)
        rank = sb("rank", [128, GROUP, 128], bf16)
        over = sb("over", [128, GROUPS])
        xT = sb("xT", [128, GROUP, 128])
        rowsum = sb("rowsum", [128, GROUP, 128])
        base0 = sb("base0", [128, GROUP, 128])
        base1 = sb("base1", [128, GROUP, 128])
        take = sb("take", [128, GROUP, SLOTS], bf16)
        W = sb("W", [128, GROUP, WOFF[-1]])
        uv = [sb(f"uv{i}", [128, 2 * D]) for i in range(2)]
        uvrest = [sb(f"uvrest{i}", [128, 2 * D]) for i in range(2)]
        parts = sb("parts", [128, SLOTS_PER_GROUP, 3, 2 * D], bf16)
        ustack = sb("ustack", [96, SLOTS_PER_GROUP, BLOCKS, D], bf16)
        m = [sb(f"m{i}", [128, 4, D]) for i in range(3)]
        sT = [sb(f"sT{i}", [128, 128]) for i in range(2)]
        hT = sb("hT", [128, GROUP, 128])
        hsum = sb("hsum", [128, GROUP, 128])
        yT = [sb(f"yT{i}", [128, 128]) for i in range(2)]
        yp = [sb(f"yp{i}", [128, 128]) for i in range(2)]
        y = sb("y", [128, GROUP, D])
        stats = sb("stats", [128, GROUP, 6])
        meanvar = sb("meanvar", [128, GROUP, 2])
        varE = sb("varE", [128, GROUP])
        rstd = sb("rstd", [128, GROUP])
        root, inv, quot, twice, half = [sb(n, [128, GROUP]) for n in "root inv quot twice half".split()]
        outs = sb("outs", [128, GROUP, D])

        Z = [ctx.enter_context(nc.psum_tensor(f"Z{i}", [128, 4, D], f32)) for i in range(3)]
        PS = ctx.enter_context(nc.psum_tensor("PS", [128, 512], f32))
        PU = ctx.enter_context(nc.psum_tensor("PU", [128, 512], f32))
        PM = ctx.enter_context(nc.psum_tensor("PM", [128, 512], f32))
        PA = ctx.enter_context(nc.psum_tensor("PA", [128, GROUP, 128], f32))
        PB = ctx.enter_context(nc.psum_tensor("PB", [128, GROUP, 128], f32))

        const_in, w_in, loaded, outs_free = map(sem, ["const_in", "w_in", "loaded", "outs_free"])
        stacked = [sem(f"stacked{s}") for s in range(SLOTS_PER_GROUP)]
        spilled = [sem(f"spilled{s}") for s in range(SLOTS_PER_GROUP)]
        bounce = [nc.dram_tensor(f"bounce{s}", (NODES * 3, D), bf16, kind="Internal").ap()
                  for s in range(SLOTS_PER_GROUP)]
        (wT_done, key_done, permT_done, adj1_done, adj2_done, rank_done, rowsum_done, xT_done, value_done, uv_done,
         z_done, sum_done, msg_done, yp_done, y_done) = [sem(f"pe_{s}") for s in (
            "wT key permT adj1 adj2 rank rowsum xT value uv z sum msg yp y".split())]
        (deg_ok, key_ok, diag_ok, above_ok, place_ok, perm_ok, nz_ok, adjrest_ok, adjlo_ok, rank_ok, over_ok, base_ok,
         take_ok, W_ok, uvsum_ok, uvrest_ok, uvlo_ok, hT_ok, hsum_ok, stats_ok, mv_ok, varE_ok, outs_ok,
         inv_ok, quot_ok, twice_ok, half_ok, rstd_ok) = [sem(f"dve_{s}") for s in (
            "deg key diag above place perm nz adjrest adjlo rank over base take W uvsum uvrest uvlo hT hsum "
            "stats mv varE outs inv quot twice half rstd".split())]
        (wT_ok, permT_ok, adj1_ok, adj2_ok, adjhi_ok, adjmid_ok, rowsum_ok, xT_ok, uvhi_ok, uvmid_ok, m_ok, sT_ok,
         yp_ok, y_ok, root_ok, table_ok) = [sem(f"act_{s}") for s in (
            "wT permT adj1 adj2 adjhi adjmid rowsum xT uvhi uvmid m sT yp y root table".split())]

        spread = sb("spread", [128, 4, D])
        pairs = sb("pairs", [128, 4, D])
        messages = sb("messages", [128, 4, D])
        uvg = sb("uvg", [128, 2 * D])
        baseg = sb("baseg", [128, 128])
        onesf = sb("onesf", [128, 128])
        overs = sb("overs", [128, 1])
        some = sb("some", [128, 1], bf16)
        flag = sb("flag", [128, 1], mybir.dt.int32)
        (overs_ok, some_ok, count_done, flag_ok) = [sem(s) for s in "dve_overs dve_some pe_count dve_flag".split()]
        (g_loaded, g_turned, g_turned_ok, g_uv, g_uv_ok, g_spread_ok, g_rows, g_pairs_ok, g_messages_ok, g_sum, g_sT_ok,
         g_base_ok, g_msg, g_h_ok, g_back, g_y_ok, g_stats_ok, g_mv_ok, g_var_ok, g_root_ok, g_out_ok, g_stored,
         onesf_ok) = [sem(f"general_{s}") for s in (
            "loaded turned turned_ok uv uv_ok spread_ok rows pairs_ok messages_ok sum sT_ok base_ok msg h_ok back y_ok "
            "stats_ok mv_ok var_ok root_ok out_ok stored ones".split())]
        STEPS = NODES // 4

        def overflow(eng):
            eng.wait_ge(flag_ok, 1)
            return eng.value_load(flag[0:1, 0:1], min_val=0, max_val=128)

        x_v = x.rearrange("b n d -> n b d")
        adj_v = adj.rearrange("b n j -> n b j")
        out_v = out.rearrange("b n d -> n b d")
        block = ctx.enter_context(nc.Block())

        @block.sync
        def _(sp):
            def start_of(g):
                return g * GROUP if isinstance(g, int) else sp.snap(g * GROUP)

            def load(g, at):
                sp.wait_ge(adj1_done, g)
                sp.wait_ge(xT_done, g)
                sp.dma_start(adj_in[:, :, :], adj_v[:, bass.ds(at, GROUP), :]).then_inc(loaded, 16)
                sp.dma_start(x_in[:, :, :], x_v[:, bass.ds(at, GROUP), :]).then_inc(loaded, 16)

            def stack(g, s):
                k = g * SLOTS_PER_GROUP + s
                sp.wait_ge(uvlo_ok, k + 1)
                sp.wait_ge(uvhi_ok, k + 1)
                sp.wait_ge(uvmid_ok, k + 1)
                sp.dma_start(bounce[s].rearrange("(i p) d -> i p d", p=3), parts[:, s, :, 0:D]).then_inc(spilled[s], 16)
                sp.wait_ge(spilled[s], 16 * (g + 1))
                sp.dma_start(ustack[:, s, :, :], bounce[s].rearrange("(b k) d -> k b d", b=BLOCKS)).then_inc(stacked[s], 16)

            def store(g, at):
                sp.wait_ge(outs_ok, g + 1)
                sp.dma_start(out_v[:, bass.ds(at, GROUP), :], outs[:, :, :]).then_inc(outs_free, 16)

            def group(g, first=False, last=False, load_next=True):
                before = 0 if first else start_of(g - 1)
                after = start_of(g + 2)
                for q in range(GROUP):
                    stack(g, GROUP + q)
                    if q == 0 and not first:
                        store(g - 1, before)
                if load_next:
                    load(g + 2, after)
                if not last:
                    for q in range(GROUP):
                        stack(g + 1, q)

            sp.dma_start(CF[:, :], cf[:, :]).then_inc(const_in, 16)
            sp.dma_start(CB[:, :].bitcast(u16), cb[:, :]).then_inc(const_in, 16)
            load(0, 0)
            sp.dma_start(w1_in[:, :, :], w1.rearrange("l o c -> o l c")).then_inc(w_in, 16)
            sp.dma_start(w2_in[:, :, :], w2.rearrange("l o c -> o l c")).then_inc(w_in, 16)
            sp.dma_start(b1row[:, :, :], b1.rearrange("(a l) d -> a l d", a=1).broadcast_to((128, LAYERS, D)))\
              .then_inc(w_in, 16)
            sp.dma_start(b2col[:, :], b2.rearrange("l d -> d l"), allow_slow_non_contiguous=True).then_inc(w_in, 16)
            load(1, GROUP)
            for q in range(GROUP):
                stack(0, q)
            group(0, first=True)
            with sp.Fori(1, GROUPS - 2) as g:
                group(g)
            group(GROUPS - 2, load_next=False)
            group(GROUPS - 1, last=True, load_next=False)
            store(GROUPS - 1, GRAPHS - GROUP)
            sp.wait_ge(outs_free, 16 * (GROUPS + 1))

            def general(b):
                at = sp.snap(b)
                sp.dma_start(adj_in[:, 0, :], adj_v[:, bass.ds(at, 1), :].rearrange("n b j -> n (b j)")).then_inc(g_loaded, 16)
                sp.dma_start(x_in[:, 0, :], x_v[:, bass.ds(at, 1), :].rearrange("n b d -> n (b d)")).then_inc(g_loaded, 16)
                sp.wait_ge(g_out_ok, b + 1)
                sp.dma_start(out_v[:, bass.ds(at, 1), :].rearrange("n b d -> n (b d)"), outs[:, 0, :]).then_inc(g_stored, 16)

            with sp.If(overflow(sp) > 0):
                with sp.Fori(0, GRAPHS) as b:
                    general(b)
                sp.wait_ge(g_stored, 16 * (GRAPHS + 1))

        @block.tensor
        def _(pe):
            mm = nc.tensor.matmul

            def z_unit(g, n):
                s, k = divmod(n, QUADS)
                q = s % GROUP
                if k == 0:
                    pe.wait_ge(uvlo_ok, g * SLOTS_PER_GROUP + s + 1)
                    pe.wait_ge(uvhi_ok, g * SLOTS_PER_GROUP + s + 1)
                    pe.wait_ge(uvmid_ok, g * SLOTS_PER_GROUP + s + 1)
                    pe.wait_ge(stacked[s], 16 * (g + 1))
                    if s < GROUP:
                        pe.wait_ge(take_ok, g * GROUP + q + 1)
                total = g * UNITS + n
                if n >= 3 or not isinstance(g, int) or g:
                    pe.wait_ge(m_ok, total - 2)
                for t in range(4 * k, min(4 * k + 4, TILES)):
                    o = Z[n % 3][:, t % 4, :]
                    lhs = take[:, q, 128 * t:128 * t + 128]
                    for p in range(3):
                        mm(o, lhs, parts[:, s, p, D:2 * D], start=(p == 0), stop=False)
                    mine = [i for i, (tt, _) in enumerate(PAIRS) if tt == t]
                    for i in mine:
                        last = mm(o, pick[0:96, i, :], ustack[:, s, PAIRS[i][1], :], start=False, stop=(i == mine[-1]))
                last.then_inc(z_done, 1)

            def sum_unit(g, n):
                s, k = divmod(n, QUADS)
                q = s % GROUP
                pe.wait_ge(m_ok, g * UNITS + n + 1)
                if k == 0:
                    pe.wait_ge(W_ok, g * GROUP + q + 1)
                    pe.wait_ge(sT_ok, g * SLOTS_PER_GROUP + s)
                for t in range(4 * k, min(4 * k + 4, TILES)):
                    lo, hi = WINDOWS[t]
                    last = mm(PS[:, lo:hi], m[n % 3][:, t % 4, :], W[:, q, WOFF[t]:WOFF[t + 1]],
                              start=(t == 0), stop=(t == TILES - 1), skip_group_check=True)
                last.then_inc(sum_done, 1)

            def msg(g, s):
                pe.wait_ge(sT_ok, g * SLOTS_PER_GROUP + s + 1)
                if 1 <= s <= GROUP:
                    pe.wait_ge(hT_ok, g * SLOTS_PER_GROUP + s)
                else:
                    pe.wait_ge(y_ok, g * GROUP + max(0, s - GROUP))
                mm(PM[:, 0:128], w2T[:, s // GROUP, :], sT[s % 2][:, :], start=True, stop=True).then_inc(msg_done, 1)

            def yp_step(g, q):
                pe.wait_ge(hT_ok, g * SLOTS_PER_GROUP + GROUP + q + 1)
                nc.tensor.transpose(PM[:, 0:128], yT[q % 2][:, :], ident).then_inc(yp_done, 1)

            def y_step(g, q):
                pe.wait_ge(yp_ok, g * GROUP + q + 1)
                if q == 0:
                    pe.wait_ge(permT_ok, g + 1)
                mm(PM[:, 0:128], permT[:, q, :], yp[q % 2][:, :], start=True, stop=True).then_inc(y_done, 1)

            def uv_step(g, s):
                k = g * SLOTS_PER_GROUP + s
                pe.wait_ge(uvsum_ok, k)
                if s < GROUP:
                    pe.wait_ge(xT_ok, g + 1)
                    h = xT
                else:
                    pe.wait_ge(hT_ok, k - GROUP + 1)
                    h = hT
                mm(PU[:, 0:2 * D], h[:, s % GROUP, :], w1T[:, s // GROUP, :], start=True, stop=True)\
                    .then_inc(uv_done, 1)

            def key_step(g):
                pe.wait_ge(diag_ok, g + 1)
                pe.wait_ge(W_ok, max(0, (g - 1) * GROUP + 3) if isinstance(g, int) else (g - 1) * GROUP + 3)
                o = PA[:, :, :].rearrange("p q i -> p (q i)")
                mm(o, onesb, degdiag[:, :, :].rearrange("p q i -> p (q i)"), start=True, stop=False)
                mm(o, onesb, tiediag, start=False, stop=True).then_inc(key_done, 1)

            def permT_step(g):
                pe.wait_ge(perm_ok, g + 1)
                pe.wait_ge(W_ok, g * GROUP + 4)
                for q in range(GROUP):
                    last = nc.tensor.transpose(PB[:, q, :], perm[:, q, :], ident)
                last.then_inc(permT_done, 1)

            def adj1_step(g):
                pe.wait_ge(perm_ok, g + 1)
                pe.wait_ge(above_ok, g + 1)
                for q in range(GROUP):
                    last = mm(PA[:, q, :], adj_in[:, q, :], perm[:, q, :], start=True, stop=True)
                last.then_inc(adj1_done, 1)

            def adj2_step(g):
                pe.wait_ge(adj1_ok, g + 1)
                for q in range(GROUP):
                    last = mm(PA[:, q, :], perm[:, q, :], adj1[:, q, :], start=True, stop=True)
                last.then_inc(adj2_done, 1)

            def rank_step(g):
                pe.wait_ge(nz_ok, g + 1)
                pe.wait_ge(permT_ok, g)
                mm(PB[:, :, :].rearrange("p q i -> p (q i)"), upto, nz[:, :, :].rearrange("p q i -> p (q i)"),
                   start=True, stop=True).then_inc(rank_done, 1)

            def rowsum_step(g):
                pe.wait_ge(adjlo_ok, g + 1)
                pe.wait_ge(adjhi_ok, g + 1)
                pe.wait_ge(adjmid_ok, g + 1)
                pe.wait_ge(adj2_ok, g + 1)
                for p in range(3):
                    last = mm(PA[:, :, :].rearrange("p q i -> p (q i)"), onesb,
                              adjp[:, p, :, :].rearrange("p q i -> p (q i)"), start=(p == 0), stop=(p == 2))
                last.then_inc(rowsum_done, 1)

            def xT_step(g):
                pe.wait_ge(perm_ok, g + 1)
                pe.wait_ge(over_ok, g + 1)
                for q in range(GROUP):
                    last = mm(PB[:, q, :], x_in[:, q, :], perm[:, q, :], start=True, stop=True)
                last.then_inc(xT_done, 1)

            def value_step(g, q):
                pe.wait_ge(take_ok, g * GROUP + q + 1)
                if q == 0:
                    pe.wait_ge(rowsum_ok, g + 1)
                elif q == 1:
                    pe.wait_ge(xT_ok, g + 1)
                else:
                    pe.wait_ge(W_ok, g * GROUP + q - 1)
                bank = (PA, PB)[q % 2][:, :, :].rearrange("p q i -> p (q i)")
                for t, (lo, hi) in enumerate(WINDOWS):
                    for p in range(3):
                        last = mm(bank[:, WOFF[t]:WOFF[t + 1]], take[:, q, 128 * t:128 * t + 128],
                                  adjp[:, p, q, lo:hi], start=(p == 0), stop=(p == 2))
                last.then_inc(value_done, 1)

            def group(g, first=False, last=False):
                for n in range(UNITS):
                    z_unit(g, n)
                    if n:
                        sum_unit(g, n - 1)
                    elif not first:
                        sum_unit(g - 1, UNITS - 1)
                    if n == 0 and not first: y_step(g - 1, 2)
                    if n == 1 and not first: msg(g - 1, 7)
                    if n == 2 and not first: yp_step(g - 1, 3)
                    if n == 2: value_step(g, 3)
                    if n == 3 and not first: y_step(g - 1, 3)
                    if n == 4 and not last: key_step(g + 1)
                    if n == 4: msg(g, 0)
                    if n == 5: permT_step(g)
                    if n == 5: uv_step(g, 4)
                    if n == 7: msg(g, 1)
                    if n == 8 and last:
                        pe.wait_ge(some_ok, 1)
                        pe.wait_ge(W_ok, g * GROUP + 3)
                        mm(PA[:, 0, 0:1], onesb, some[:, :], start=True, stop=True).then_inc(count_done, 1)
                    if n == 7 and not last: adj1_step(g + 1)
                    if n == 8: uv_step(g, 5)
                    if n == 9 and not last: adj2_step(g + 1)
                    if n == 10: msg(g, 2)
                    if n == 11: uv_step(g, 6)
                    if n == 11 and not last: rank_step(g + 1)
                    if n == 13: msg(g, 3)
                    if n == 14: uv_step(g, 7)
                    if n == 15 and not last: rowsum_step(g + 1)
                    if n == 16: msg(g, 4)
                    if n == 16 and not last: xT_step(g + 1)
                    if n == 17: yp_step(g, 0)
                    if n == 17 and not last: value_step(g + 1, 0)
                    if n == 18: y_step(g, 0)
                    if n == 18 and not last: uv_step(g + 1, 0)
                    if n == 19: msg(g, 5)
                    if n == 20: yp_step(g, 1)
                    if n == 20 and not last: value_step(g + 1, 1)
                    if n == 20 and not last: uv_step(g + 1, 1)
                    if n == 21: y_step(g, 1)
                    if n == 21 and not last: uv_step(g + 1, 2)
                    if n == 22: msg(g, 6)
                    if n == 23: yp_step(g, 2)
                    if n == 23 and not last: value_step(g + 1, 2)
                    if n == 23 and not last: uv_step(g + 1, 3)

            pe.wait_ge(const_in, 32)
            pe.wait_ge(w_in, 64)
            for l in range(LAYERS):
                nc.tensor.transpose(PA[:, 2 * l, :], w1_in[:, l, 0:D], ident)
                nc.tensor.transpose(PA[:, 2 * l + 1, :], w1_in[:, l, D:2 * D], ident)
            for l in range(LAYERS):
                last = nc.tensor.transpose(PB[:, l, :], w2_in[:, l, :], ident)
            last.then_inc(wT_done, 1)
            pe.wait_ge(wT_ok, 2)
            key_step(0)
            adj1_step(0)
            adj2_step(0)
            rank_step(0)
            rowsum_step(0)
            xT_step(0)
            for q in range(GROUP):
                uv_step(0, q)
                if q < 3:
                    value_step(0, q)
            group(0, first=True)
            with pe.Fori(1, GROUPS - 1) as g:
                group(g)
            group(GROUPS - 1, last=True)
            g = GROUPS - 1
            sum_unit(g, UNITS - 1)
            y_step(g, 2)
            msg(g, 7)
            yp_step(g, 3)
            y_step(g, 3)

            def general(b):
                pe.wait_ge(g_loaded, 32 * (b + 1))
                nc.tensor.transpose(PA[:, 0, :], adj_in[:, 0, :], ident)
                nc.tensor.transpose(PA[:, 1, :], x_in[:, 0, :], ident).then_inc(g_turned, 1)
                pe.wait_ge(g_turned_ok, 2 * b + 1)
                mm(PA[:, 2, :], onesf[:, :], adj1[:, 0, :], start=True, stop=True).then_inc(g_turned, 1)
                for l in range(LAYERS):
                    h = (xT, hT)[l]
                    if l == 0:
                        pe.wait_ge(g_turned_ok, 2 * b + 2)
                    else:
                        pe.wait_ge(g_h_ok, 2 * b + 1)
                    mm(PU[:, 0:2 * D], h[:, 0, :], w1T[:, l, :], start=True, stop=True).then_inc(g_uv, 1)
                    with pe.Fori(0, STEPS) as i:
                        n = (b * LAYERS + l) * STEPS + i + 1
                        pe.wait_ge(g_spread_ok, n)
                        mm(Z[0][:, :, :].rearrange("p r d -> p (r d)"), onesf[:, :],
                           spread[:, :, :].rearrange("p r d -> p (r d)"), start=True, stop=True).then_inc(g_rows, 1)
                        pe.wait_ge(g_messages_ok, n)
                        for r in range(4):
                            last = mm(PS[:, bass.ds(4 * i + r, 1)], messages[:, r, :], adj1[:, 0, bass.ds(4 * i + r, 1)],
                                      start=True, stop=True)
                        last.then_inc(g_sum, 1)
                    pe.wait_ge(g_sT_ok, 2 * b + l + 1)
                    mm(PM[:, 0:128], w2T[:, l, :], sT[0][:, :], start=True, stop=True).then_inc(g_msg, 1)
                pe.wait_ge(g_h_ok, 2 * b + 2)
                nc.tensor.transpose(PM[:, 0:128], hT[:, 0, :], ident).then_inc(g_back, 1)

            with pe.If(overflow(pe) > 0):
                pe.wait_ge(onesf_ok, 1)
                with pe.Fori(0, GRAPHS) as b:
                    general(b)

        @block.scalar
        def _(act):
            def copy(o, i):
                return nc.scalar.activation(o, i, ACT.Copy)

            def relu_unit(g, n):
                total = g * UNITS + n
                act.wait_ge(z_done, total + 1)
                if n >= 3 or not isinstance(g, int) or g:
                    act.wait_ge(sum_done, total - 2)
                tiles = min(4, TILES - n % QUADS * 4)
                nc.scalar.activation(m[n % 3][:, 0:tiles, :], Z[n % 3][:, 0:tiles, :], ACT.Relu).then_inc(m_ok, 1)

            def sT_step(g, s):
                act.wait_ge(sum_done, g * UNITS + (s + 1) * QUADS)
                k = g * SLOTS_PER_GROUP + s
                if s >= 2 or not isinstance(g, int) or g:
                    act.wait_ge(msg_done, k - 1)
                copy(sT[s % 2][:, :], PS[:, 0:128]).then_inc(sT_ok, 1)

            def yp_copy(g, q):
                act.wait_ge(yp_done, g * GROUP + q + 1)
                if q >= 2 or not isinstance(g, int) or g:
                    act.wait_ge(y_done, g * GROUP + q - 1)
                copy(yp[q % 2][:, :], PM[:, 0:128]).then_inc(yp_ok, 1)

            def y_copy(g, q):
                act.wait_ge(y_done, g * GROUP + q + 1)
                if q == 0:
                    act.wait_ge(outs_ok, g)
                copy(y[:, q, :], PM[:, 0:128]).then_inc(y_ok, 1)

            def hi_step(g, s):
                k = g * SLOTS_PER_GROUP + s
                act.wait_ge(uvsum_ok, k + 1)
                if not isinstance(g, int) or g:
                    act.wait_ge(z_done, (g - 1) * UNITS + (s + 1) * QUADS)
                    act.wait_ge(stacked[s], 16 * g)
                copy(parts[:, s, 0, :], uv[s % 2][:, :]).then_inc(uvhi_ok, 1)

            def mid_step(g, s):
                act.wait_ge(uvrest_ok, g * SLOTS_PER_GROUP + s + 1)
                copy(parts[:, s, 1, :], uvrest[s % 2][:, :]).then_inc(uvmid_ok, 1)

            def permT_copy(g):
                act.wait_ge(permT_done, g + 1)
                act.wait_ge(y_done, g * GROUP)
                copy(permT[:, :, :], PB[:, :, :]).then_inc(permT_ok, 1)

            def adj1_copy(g):
                act.wait_ge(adj1_done, g + 1)
                act.wait_ge(adj2_done, g)
                copy(adj1[:, :, :], PA[:, :, :]).then_inc(adj1_ok, 1)

            def adj2_copy(g):
                act.wait_ge(adj2_done, g + 1)
                act.wait_ge(nz_ok, g)
                act.wait_ge(adjrest_ok, g)
                copy(adj2[:, :, :], PA[:, :, :]).then_inc(adj2_ok, 1)

            def adjhi_step(g):
                act.wait_ge(adj2_ok, g + 1)
                act.wait_ge(value_done, g * GROUP)
                act.wait_ge(rowsum_done, g)
                copy(adjp[:, 0, :, :], adj2[:, :, :]).then_inc(adjhi_ok, 1)

            def adjmid_step(g):
                act.wait_ge(adjrest_ok, g + 1)
                copy(adjp[:, 1, :, :], adjrest[:, :, :]).then_inc(adjmid_ok, 1)

            def rowsum_copy(g):
                act.wait_ge(rowsum_done, g + 1)
                act.wait_ge(base_ok, 2 * g)
                copy(rowsum[:, :, :], PA[:, :, :]).then_inc(rowsum_ok, 1)

            def xT_copy(g):
                act.wait_ge(xT_done, g + 1)
                act.wait_ge(base_ok, 2 * g)
                act.wait_ge(uv_done, g * SLOTS_PER_GROUP)
                copy(xT[:, :, :], PB[:, :, :]).then_inc(xT_ok, 1)

            def root_step(g):
                act.wait_ge(varE_ok, g + 1)
                nc.scalar.activation(root[:, :], varE[:, :], ACT.Sqrt).then_inc(root_ok, 1)

            def group(g, first=False, last=False):
                for n in range(UNITS):
                    relu_unit(g, n)
                    if n == 0 and not first: sT_step(g - 1, 7)
                    if n == 0 and not first: y_copy(g - 1, 2)
                    if n == 2 and not first: yp_copy(g - 1, 3)
                    if n == 3 and not first: y_copy(g - 1, 3)
                    if n % QUADS == 0 and n: sT_step(g, n // QUADS - 1)
                    if n == 5: permT_copy(g)
                    if n == 5: hi_step(g, 4)
                    if n == 6: mid_step(g, 4)
                    if n == 7 and not last: adj1_copy(g + 1)
                    if n == 8 and not first: root_step(g - 1)
                    if n == 8: hi_step(g, 5)
                    if n == 9: mid_step(g, 5)
                    if n == 9 and not last: adj2_copy(g + 1)
                    if n == 9 and not last: adjhi_step(g + 1)
                    if n == 10 and not last: adjmid_step(g + 1)
                    if n == 11: hi_step(g, 6)
                    if n == 12: mid_step(g, 6)
                    if n == 14: hi_step(g, 7)
                    if n == 15: mid_step(g, 7)
                    if n == 15 and not last: rowsum_copy(g + 1)
                    if n == 16 and not last: xT_copy(g + 1)
                    if n == 17: yp_copy(g, 0)
                    if n == 18: y_copy(g, 0)
                    if n == 18 and not last: hi_step(g + 1, 0)
                    if n == 19 and not last: mid_step(g + 1, 0)
                    if n == 20: yp_copy(g, 1)
                    if n == 20 and not last: hi_step(g + 1, 1)
                    if n == 21: y_copy(g, 1)
                    if n == 21 and not last: mid_step(g + 1, 1)
                    if n == 21 and not last: hi_step(g + 1, 2)
                    if n == 22 and not last: mid_step(g + 1, 2)
                    if n == 23: yp_copy(g, 2)
                    if n == 23 and not last: hi_step(g + 1, 3)
                    if n == 23 and not last: mid_step(g + 1, 3)

            act.wait_ge(const_in, 32)
            nc.scalar.activation(root[:, 0:1], iota[:, 0:1], ACT.Sqrt).then_inc(table_ok, 1)
            act.wait_ge(table_ok, 1)
            act.wait_ge(wT_done, 1)
            copy(w1T[:, :, :].rearrange("p l o -> p (l o)"), PA[:, :, :].rearrange("p q i -> p (q i)"))\
                .then_inc(wT_ok, 1)
            copy(w2T[:, :, :], PB[:, 0:2, :]).then_inc(wT_ok, 1)
            adj1_copy(0)
            adj2_copy(0)
            adjhi_step(0)
            adjmid_step(0)
            rowsum_copy(0)
            xT_copy(0)
            for q in range(GROUP):
                hi_step(0, q)
                mid_step(0, q)
            group(0, first=True)
            with act.Fori(1, GROUPS - 1) as g:
                group(g)
            group(GROUPS - 1, last=True)
            g = GROUPS - 1
            sT_step(g, 7)
            y_copy(g, 2)
            yp_copy(g, 3)
            y_copy(g, 3)
            root_step(g)

            def general(b):
                act.wait_ge(g_turned, 2 * b + 1)
                copy(adj1[:, 0, :], PA[:, 0, :]).then_inc(g_turned_ok, 1)
                act.wait_ge(g_turned, 2 * b + 2)
                copy(xT[:, 0, :], PA[:, 1, :])
                copy(rowsum[:, 0, :], PA[:, 2, :]).then_inc(g_turned_ok, 1)
                for l in range(LAYERS):
                    with act.Fori(0, STEPS) as i:
                        act.wait_ge(g_pairs_ok, (b * LAYERS + l) * STEPS + i + 1)
                        nc.scalar.activation(messages[:, :, :], pairs[:, :, :], ACT.Relu).then_inc(g_messages_ok, 1)
                    act.wait_ge(g_sum, (b * LAYERS + l + 1) * STEPS)
                    copy(sT[0][:, :], PS[:, 0:128]).then_inc(g_sT_ok, 1)
                act.wait_ge(g_back, b + 1)
                copy(y[:, 0, :], PM[:, 0:128]).then_inc(g_y_ok, 1)
                act.wait_ge(g_var_ok, b + 1)
                nc.scalar.activation(root[:, 0:1], varE[:, 0:1], ACT.Sqrt).then_inc(g_root_ok, 1)

            with act.If(overflow(act) > 0):
                with act.Fori(0, GRAPHS) as b:
                    general(b)

        @block.vector
        def _(dve):
            V = nc.vector

            def wide(a):
                return a.rearrange("p (q i) -> p q i", q=1).broadcast_to((128, GROUP, 128))

            def col(a):
                return a[:, :].rearrange("p (q i) -> p q i", i=1).broadcast_to((128, GROUP, 128))

            def deg_step(g):
                dve.wait_ge(loaded, 32 * (g + 1))
                for q in range(GROUP):
                    last = V.tensor_scalar(junk[:, q, :], adj_in[:, q, :], 0.0, None, ALU.not_equal, ALU.add,
                                           accum_out=deg[:, q:q + 1])
                last.then_inc(deg_ok, 1)
                dve.wait_ge(deg_ok, g + 1)
                V.tensor_scalar(key[:, :], deg[:, :], tie, None, ALU.add).then_inc(key_ok, 1)
                dve.wait_ge(key_done, g)
                V.tensor_tensor(degdiag[:, :, :], wide(identb), col(deg), ALU.mult).then_inc(diag_ok, 1)

            def place_step(g):
                dve.wait_ge(key_done, g + 1)
                dve.wait_ge(key_ok, g + 1)
                V.tensor_tensor(above[:, :, :], PA[:, :, :], col(key), ALU.is_gt).then_inc(above_ok, 1)
                dve.wait_ge(above_ok, g + 1)
                V.tensor_reduce(place[:, :], above[:, :, :], AX.X, ALU.add).then_inc(place_ok, 1)

            def perm_step(g):
                dve.wait_ge(place_ok, g + 1)
                dve.wait_ge(permT_done, g)
                dve.wait_ge(xT_done, g)
                V.tensor_tensor(perm[:, :, :], wide(iota), col(place), ALU.is_equal).then_inc(perm_ok, 1)

            def adj_step(g):
                dve.wait_ge(adj2_ok, g + 1)
                dve.wait_ge(rank_done, g)
                V.tensor_scalar(nz[:, :, :], adj2[:, :, :], 0.0, None, ALU.not_equal).then_inc(nz_ok, 1)
                dve.wait_ge(adjhi_ok, g + 1)
                dve.wait_ge(adjmid_ok, g)
                V.tensor_tensor(adjrest[:, :, :], adj2[:, :, :], adjp[:, 0, :, :], ALU.subtract)\
                    .then_inc(adjrest_ok, 1)

            def adjlo_step(g):
                dve.wait_ge(adjmid_ok, g + 1)
                V.tensor_tensor(adjp[:, 2, :, :], adjrest[:, :, :], adjp[:, 1, :, :], ALU.subtract)\
                    .then_inc(adjlo_ok, 1)

            def rank_step(g):
                dve.wait_ge(rank_done, g + 1)
                V.tensor_tensor(rank[:, :, :], PB[:, :, :], nz[:, :, :], ALU.mult).then_inc(rank_ok, 1)
                V.scalar_tensor_tensor(out=junk[:, :, :], in0=PB[:, :, :], scalar=0.0, in1=wide(caps),
                                       op0=ALU.add, op1=ALU.is_gt, accum_out=over[:, bass.ds(g, 1)])\
                    .then_inc(over_ok, 1)

            def base_step(g):
                dve.wait_ge(rowsum_ok, g + 1)
                dve.wait_ge(xT_ok, g + 1)
                dve.wait_ge(hsum_ok, g * GROUP)
                V.scalar_tensor_tensor(out=base0[:, :, :], in0=rowsum[:, :, :], scalar=b2col[:, 0:1],
                                       in1=xT[:, :, :], op0=ALU.mult, op1=ALU.add).then_inc(base_ok, 1)
                V.scalar_tensor_tensor(out=base1[:, :, :], in0=rowsum[:, :, :], scalar=b2col[:, 1:2],
                                       in1=xT[:, :, :], op0=ALU.mult, op1=ALU.add).then_inc(base_ok, 1)

            def take_step(g, q):
                dve.wait_ge(rank_ok, g + 1)
                if not isinstance(g, int) or g:
                    dve.wait_ge(z_done, (g - 1) * UNITS + (GROUP + q + 1) * QUADS)
                r0 = off = 0
                for rows, cap in REGIONS:
                    n = rows * cap
                    o = take[:, q, off:off + n].rearrange("p (k i) -> p k i", i=rows)
                    c = rankc[:, off:off + n].rearrange("p (k i) -> p k i", i=rows)
                    r = rank[:, q, r0:r0 + rows].rearrange("p (k i) -> p k i", k=1).broadcast_to((128, cap, rows))
                    last = V.tensor_tensor(o, r, c, ALU.is_equal)
                    r0, off = r0 + rows, off + n
                last.then_inc(take_ok, 1)

            def W_step(g, q):
                dve.wait_ge(value_done, g * GROUP + q + 1)
                if not isinstance(g, int) or g:
                    dve.wait_ge(sum_done, (g - 1) * UNITS + (GROUP + q + 1) * QUADS)
                bank = (PA, PB)[q % 2][:, :, :].rearrange("p q i -> p (q i)")
                V.tensor_tensor(W[:, q, :], bank[:, 0:WOFF[-1]], mask, ALU.mult).then_inc(W_ok, 1)

            def uv_step(g, s):
                k = g * SLOTS_PER_GROUP + s
                dve.wait_ge(uv_done, k + 1)
                if s >= 2 or not isinstance(g, int) or g:
                    dve.wait_ge(uvhi_ok, k - 1)
                    dve.wait_ge(uvrest_ok, k - 1)
                V.tensor_copy(uv[s % 2][:, D:2 * D], PU[:, D:2 * D])
                V.tensor_tensor(uv[s % 2][:, 0:D], PU[:, 0:D], b1row[:, s // GROUP, :], ALU.add)\
                    .then_inc(uvsum_ok, 1)

            def rest_step(g, s):
                k = g * SLOTS_PER_GROUP + s
                dve.wait_ge(uvhi_ok, k + 1)
                if s >= 2 or not isinstance(g, int) or g:
                    dve.wait_ge(uvlo_ok, k - 1)
                    dve.wait_ge(uvmid_ok, k - 1)
                V.tensor_tensor(uvrest[s % 2][:, :], uv[s % 2][:, :], parts[:, s, 0, :], ALU.subtract)\
                    .then_inc(uvrest_ok, 1)
                dve.wait_ge(uvmid_ok, k + 1)
                V.tensor_tensor(parts[:, s, 2, :], uvrest[s % 2][:, :], parts[:, s, 1, :], ALU.subtract)\
                    .then_inc(uvlo_ok, 1)

            def h_step(g, s):
                dve.wait_ge(msg_done, g * SLOTS_PER_GROUP + s + 1)
                q = s % GROUP
                if s < GROUP:
                    dve.wait_ge(base_ok, 2 * g + 1)
                    if q == 0:
                        dve.wait_ge(uv_done, g * SLOTS_PER_GROUP)
                    V.tensor_tensor(hT[:, q, :], PM[:, 0:128], base0[:, q, :], ALU.add).then_inc(hT_ok, 1)
                else:
                    dve.wait_ge(hsum_ok, g * GROUP + q + 1)
                    if q >= 2 or not isinstance(g, int) or g:
                        dve.wait_ge(yp_done, g * GROUP + q - 1)
                    V.tensor_tensor(yT[q % 2][:, :], PM[:, 0:128], hsum[:, q, :], ALU.add).then_inc(hT_ok, 1)

            def hsum_step(g, q):
                dve.wait_ge(hT_ok, g * SLOTS_PER_GROUP + q + 1)
                dve.wait_ge(base_ok, 2 * g + 2)
                V.tensor_tensor(hsum[:, q, :], hT[:, q, :], base1[:, q, :], ALU.add).then_inc(hsum_ok, 1)

            def norm_stats(g):
                dve.wait_ge(y_ok, (g + 1) * GROUP)
                for q in range(GROUP):
                    last = V.bn_stats(stats[:, q, :], y[:, q, :])
                last.then_inc(stats_ok, 1)
                dve.wait_ge(stats_ok, g + 1)
                V.memset(varE[:, :], 0.0)
                for q in range(GROUP):
                    last = V.bn_aggr(meanvar[:, q, :], stats[:, q, :])
                last.then_inc(mv_ok, 1)
                dve.wait_ge(mv_ok, g + 1)
                V.tensor_scalar(varE[:, :], meanvar[:, :, 1], EPS, None, ALU.add).then_inc(varE_ok, 1)

            def rstd_step(n, k):
                V.reciprocal(inv[:, 0:n], root[:, 0:n]).then_inc(inv_ok, 1)
                dve.wait_ge(inv_ok, k + 1)
                V.tensor_tensor(quot[:, 0:n], varE[:, 0:n], inv[:, 0:n], ALU.mult).then_inc(quot_ok, 1)
                dve.wait_ge(quot_ok, k + 1)
                V.tensor_tensor(twice[:, 0:n], quot[:, 0:n], root[:, 0:n], ALU.add).then_inc(twice_ok, 1)
                dve.wait_ge(twice_ok, k + 1)
                V.tensor_scalar(half[:, 0:n], twice[:, 0:n], 0.5, None, ALU.mult).then_inc(half_ok, 1)
                dve.wait_ge(half_ok, k + 1)
                V.reciprocal(rstd[:, 0:n], half[:, 0:n]).then_inc(rstd_ok, 1)
                dve.wait_ge(rstd_ok, k + 1)

            def norm_out(g):
                dve.wait_ge(root_ok, g + 1)
                rstd_step(GROUP, g)
                dve.wait_ge(outs_free, 16 * (g + 1))
                for q in range(GROUP):
                    last = V.tensor_scalar(outs[:, q, :], y[:, q, :], meanvar[:, q, 0:1], rstd[:, q:q + 1],
                                           ALU.subtract, ALU.mult)
                last.then_inc(outs_ok, 1)

            def group(g, first=False, last=False):
                for n in range(UNITS):
                    if n == 0: take_step(g, 3)
                    if n == 1 and not first: h_step(g - 1, 7)
                    if n == 2: W_step(g, 3)
                    if n == 3 and not last: deg_step(g + 1)
                    if n == 4: h_step(g, 0)
                    if n == 4 and not last: place_step(g + 1)
                    if n == 5: uv_step(g, 4)
                    if n == 5 and not last: perm_step(g + 1)
                    if n == 5 and not first: norm_stats(g - 1)
                    if n == 6 and last:
                        dve.wait_ge(over_ok, GROUPS)
                        V.tensor_reduce(overs[:, :], over[:, :], AX.X, ALU.add).then_inc(overs_ok, 1)
                        dve.wait_ge(overs_ok, 1)
                        V.tensor_scalar(some[:, :], overs[:, :], 1.0, None, ALU.min).then_inc(some_ok, 1)
                    if n == 9 and last:
                        dve.wait_ge(count_done, 1)
                        V.tensor_copy(flag[:, :], PA[:, 0, 0:1]).then_inc(flag_ok, 1)
                    if n == 6: rest_step(g, 4)
                    if n == 6: hsum_step(g, 0)
                    if n == 7: h_step(g, 1)
                    if n == 8: uv_step(g, 5)
                    if n == 9: rest_step(g, 5)
                    if n == 9 and not first: norm_out(g - 1)
                    if n == 9: hsum_step(g, 1)
                    if n == 10: h_step(g, 2)
                    if n == 10 and not last: adj_step(g + 1)
                    if n == 11: uv_step(g, 6)
                    if n == 11 and not last: adjlo_step(g + 1)
                    if n == 12: rest_step(g, 6)
                    if n == 12: hsum_step(g, 2)
                    if n == 12 and not last: rank_step(g + 1)
                    if n == 13: h_step(g, 3)
                    if n == 14: uv_step(g, 7)
                    if n == 15 and not last: take_step(g + 1, 0)
                    if n == 15: rest_step(g, 7)
                    if n == 15: hsum_step(g, 3)
                    if n == 16: h_step(g, 4)
                    if n == 17 and not last: base_step(g + 1)
                    if n == 17 and not last: W_step(g + 1, 0)
                    if n == 18 and not last: take_step(g + 1, 1)
                    if n == 18 and not last: uv_step(g + 1, 0)
                    if n == 19: h_step(g, 5)
                    if n == 19 and not last: rest_step(g + 1, 0)
                    if n == 20 and not last: W_step(g + 1, 1)
                    if n == 20 and not last: uv_step(g + 1, 1)
                    if n == 21 and not last: take_step(g + 1, 2)
                    if n == 21 and not last: rest_step(g + 1, 1)
                    if n == 21 and not last: uv_step(g + 1, 2)
                    if n == 22: h_step(g, 6)
                    if n == 22 and not last: rest_step(g + 1, 2)
                    if n == 23 and not last: W_step(g + 1, 2)
                    if n == 23 and not last: uv_step(g + 1, 3)
                    if n == 23 and not last: rest_step(g + 1, 3)

            V.memset(outs[:, :, :], 0.0).then_inc(outs_free, 16)
            dve.wait_ge(const_in, 32)
            dve.wait_ge(w_in, 64)
            deg_step(0)
            place_step(0)
            perm_step(0)
            adj_step(0)
            adjlo_step(0)
            rank_step(0)
            for q in range(3):
                take_step(0, q)
            base_step(0)
            for q in range(GROUP):
                uv_step(0, q)
                if q < 3:
                    W_step(0, q)
                rest_step(0, q)
            group(0, first=True)
            with dve.Fori(1, GROUPS - 1) as g:
                group(g)
            group(GROUPS - 1, last=True)
            g = GROUPS - 1
            h_step(g, 7)
            norm_stats(g)
            norm_out(g)

            def general(b):
                for l in range(LAYERS):
                    dve.wait_ge(g_uv, 2 * b + l + 1)
                    V.tensor_tensor(uvg[:, 0:D], PU[:, 0:D], b1row[:, l, :], ALU.add)
                    V.tensor_copy(uvg[:, D:2 * D], PU[:, D:2 * D]).then_inc(g_uv_ok, 1)
                    with dve.Fori(0, STEPS) as i:
                        dve.wait_ge(g_uv_ok, 2 * b + l + 1)
                        n = (b * LAYERS + l) * STEPS + i + 1
                        u = uvg[:, 0:D].rearrange("p (r d) -> p r d", r=1).broadcast_to((128, 4, D))
                        pickrow = ident[:, bass.ds(4 * i, 4)].rearrange("p (r d) -> p r d", d=1).broadcast_to((128, 4, D))
                        V.tensor_tensor(spread[:, :, :], u, pickrow, ALU.mult).then_inc(g_spread_ok, 1)
                        dve.wait_ge(g_rows, n)
                        v = uvg[:, D:2 * D].rearrange("p (r d) -> p r d", r=1).broadcast_to((128, 4, D))
                        V.tensor_tensor(pairs[:, :, :], Z[0][:, :, :], v, ALU.add).then_inc(g_pairs_ok, 1)
                    h = (xT, hT)[l]
                    V.scalar_tensor_tensor(out=baseg[:, :], in0=rowsum[:, 0, :], scalar=b2col[:, l:l + 1],
                                           in1=h[:, 0, :], op0=ALU.mult, op1=ALU.add).then_inc(g_base_ok, 1)
                    dve.wait_ge(g_base_ok, 3 * b + l + 1)
                    if l == 1:
                        V.tensor_tensor(baseg[:, :], baseg[:, :], xT[:, 0, :], ALU.add).then_inc(g_base_ok, 1)
                        dve.wait_ge(g_base_ok, 3 * b + 3)
                    dve.wait_ge(g_msg, 2 * b + l + 1)
                    V.tensor_tensor(hT[:, 0, :], PM[:, 0:128], baseg[:, :], ALU.add).then_inc(g_h_ok, 1)
                dve.wait_ge(g_y_ok, b + 1)
                V.bn_stats(stats[:, 0, :], y[:, 0, :]).then_inc(g_stats_ok, 1)
                dve.wait_ge(g_stats_ok, b + 1)
                V.memset(varE[:, :], 0.0)
                V.bn_aggr(meanvar[:, 0, :], stats[:, 0, :]).then_inc(g_mv_ok, 1)
                dve.wait_ge(g_mv_ok, b + 1)
                V.tensor_scalar(varE[:, 0:1], meanvar[:, 0, 1:2], EPS, None, ALU.add).then_inc(g_var_ok, 1)
                dve.wait_ge(g_root_ok, b + 1)
                rstd_step(1, GROUPS + b)
                dve.wait_ge(g_stored, 16 * (b + 1))
                V.tensor_scalar(outs[:, 0, :], y[:, 0, :], meanvar[:, 0, 0:1], rstd[:, 0:1],
                                ALU.subtract, ALU.mult).then_inc(g_out_ok, 1)

            with dve.If(overflow(dve) > 0):
                dve.wait_ge(outs_free, 16 * (GROUPS + 1))
                V.memset(onesf[:, :], 1.0).then_inc(onesf_ok, 1)
                V.memset(outs[:, 0, :], 0.0).then_inc(g_stored, 16)
                with dve.Fori(0, GRAPHS) as b:
                    general(b)


_INS = ['x', 'adj', 'L0_gnn_w1', 'L0_gnn_b1', 'L0_gnn_w2', 'L0_gnn_b2']


def kernel(**inputs):
    import numpy as _np
    import concourse.bacc as _bacc
    from concourse import mybir as _mybir
    from concourse.bass_utils import run_bass_kernel_spmd as _run

    nc = _bacc.Bacc("TRN2", target_bir_lowering=False, num_devices=1)
    cf, cb = constants()
    arrays, args = {}, []
    for name, a in [(n, inputs[n]) for n in _INS] + [('tables_f32', cf), ('tables_bf16', cb)]:
        a = _np.ascontiguousarray(a)
        arrays[f"in_{name}_dram"] = a
        args.append(nc.dram_tensor(f"in_{name}_dram", a.shape, _mybir.dt.from_np(a.dtype), kind="ExternalInput").ap())
    out = nc.dram_tensor("out_0_dram", (GRAPHS, NODES, D), _mybir.dt.float32, kind="ExternalOutput").ap()
    gnn_kernel(nc, *args, out)
    r = _run(nc, [arrays], core_ids=[0])
    return r.results[0]["out_0_dram"]
```

```python
import numpy as np
import concourse.bass as bass
from concourse import mybir
from contextlib import ExitStack


NODES = 128
D = 128
GRAPHS = 64
LAYERS = 2
GROUP = 4
GROUPS = GRAPHS // GROUP
EPS = 1e-5

REGIONS = [(2, 26), (6, 18), (8, 15), (8, 14), (8, 13), (16, 12), (16, 11), (16, 10), (16, 9), (16, 8), (16, 7)]
SLOTS = sum(r * c for r, c in REGIONS)
TILES = SLOTS // 128
QUADS = -(-TILES // 4)
BLOCKS = NODES // 32
SLOTS_PER_GROUP = 2 * GROUP
UNITS = SLOTS_PER_GROUP * QUADS
assert sum(r for r, _ in REGIONS) == NODES and SLOTS % 128 == 0


def slot_rows():
    rows, ranks, r0 = [], [], 0
    for n, cap in REGIONS:
        for k in range(cap):
            for i in range(n):
                rows.append(r0 + i)
                ranks.append(k)
        r0 += n
    return np.array(rows), np.array(ranks)


ROWS, RANKS = slot_rows()
WINDOWS = [(int(ROWS[128 * t:128 * t + 128].min()), int(ROWS[128 * t:128 * t + 128].max()) + 1) for t in range(TILES)]
WOFF = [sum(hi - lo for lo, hi in WINDOWS[:t]) for t in range(TILES + 1)]
SPLIT = 4
SPLIT_ROWS = max(hi for _, hi in WINDOWS[:SPLIT])
SPLIT_W = 3 * WOFF[SPLIT]
WHOLE_W = WOFF[-1] - WOFF[SPLIT]
assert QUADS == 3 and SPLIT_W + WHOLE_W <= 512
PAIRS = [(t, b) for t in range(TILES) for b in range(WINDOWS[t][0] // 32, (WINDOWS[t][1] - 1) // 32 + 1)]


def constants():
    def bits(a):
        return (np.ascontiguousarray(a, np.float32).view(np.uint32) >> 16).astype(np.uint16)
    p = np.arange(128)
    caps = np.zeros(128)
    np.maximum.at(caps, ROWS, RANKS + 1)
    mask = np.zeros((128, SPLIT_W + WHOLE_W))
    for t, (lo, hi) in enumerate(WINDOWS):
        row = ROWS[128 * t:128 * t + 128] - lo
        if t < SPLIT:
            for part in range(3):
                mask[p, 3 * WOFF[t] + part * (hi - lo) + row] = 1
        else:
            mask[p, SPLIT_W + WOFF[t] - WOFF[SPLIT] + row] = 1
    pick = np.zeros((128, len(PAIRS), 128))
    for n, (t, b) in enumerate(PAIRS):
        for e in range(128):
            r = ROWS[128 * t + e] - 32 * b
            if 0 <= r < 32:
                pick[3 * r:3 * r + 3, n, e] = 1
    tie = (127 - p) / 128
    f = [np.eye(128), np.broadcast_to(p, (128, 128)), np.broadcast_to(caps, (128, 128)), tie[:, None], mask]
    b = [np.eye(128), np.triu(np.ones((128, 128))), np.ones((128, 128)), np.tile(np.diag(tie), (1, GROUP)),
         np.broadcast_to(RANKS + 1, (128, SLOTS)), pick.reshape(128, -1)]
    return (np.concatenate([np.asarray(a, np.float32) for a in f], 1),
            np.concatenate([bits(a) for a in b], 1))


def gnn_kernel(nc, x, adj, w1, b1, w2, b2, cf, cb, out):
    f32, bf16, u16 = mybir.dt.float32, mybir.dt.bfloat16, mybir.dt.uint16
    ALU, ACT, AX = mybir.AluOpType, mybir.ActivationFunctionType, mybir.AxisListType
    ctx = ExitStack()
    with ctx:
        def sb(name, shape, dt=f32):
            return ctx.enter_context(nc.sbuf_tensor(name, shape, dt))

        def sem(name):
            return ctx.enter_context(nc.semaphore(name))

        CF = sb("CF", [128, cf.shape[1]])
        CB = sb("CB", [128, cb.shape[1]], bf16)
        ident, iota, caps, tie = CF[:, 0:128], CF[:, 128:256], CF[:, 256:384], CF[:, 384:385]
        mask = CF[:, 385:385 + SPLIT_W + WHOLE_W]
        identb, upto, onesb, tiediag = CB[:, 0:128], CB[:, 128:256], CB[:, 256:384], CB[:, 384:384 + 512]
        rankc = CB[:, 896:896 + SLOTS]
        pick = CB[:, 896 + SLOTS:].rearrange("p (n e) -> p n e", e=128)
        w1_in = sb("w1_in", [128, LAYERS, 2 * D])
        w2_in = sb("w2_in", [128, LAYERS, D])
        w1T = sb("w1T", [128, LAYERS, 2 * D])
        w2T = sb("w2T", [128, LAYERS, D])
        b1row = sb("b1row", [128, LAYERS, D])
        b2col = sb("b2col", [128, LAYERS])

        adj_in = sb("adj_in", [128, GROUP, NODES])
        x_in = sb("x_in", [128, GROUP, D])
        junk = sb("junk", [128, GROUP, 128], bf16)
        deg = sb("deg", [128, GROUP])
        key = sb("key", [128, GROUP])
        degdiag = sb("degdiag", [128, GROUP, 128], bf16)
        above = sb("above", [128, GROUP, 128], bf16)
        place = sb("place", [128, GROUP])
        perm = sb("perm", [128, GROUP, 128])
        permT = sb("permT", [128, GROUP, 128])
        adj1 = sb("adj1", [128, GROUP, 128])
        adj2 = sb("adj2", [128, GROUP, 128])
        adjrest = sb("adjrest", [128, GROUP, 128])
        adjp = sb("adjp", [128, 3, GROUP, 128], bf16)
        nz = sb("nz", [128, GROUP, 128], bf16)
        rank = sb("rank", [128, GROUP, 128], bf16)
        over = sb("over", [128, GROUPS])
        xT = sb("xT", [128, GROUP, 128])
        rowsum = sb("rowsum", [128, GROUP, 128])
        base0 = sb("base0", [128, GROUP, 128])
        base1 = sb("base1", [128, GROUP, 128])
        take = sb("take", [128, GROUP, SLOTS], bf16)
        Wparts = sb("Wparts", [128, GROUP, SPLIT_W], bf16)
        W = sb("W", [128, GROUP, WHOLE_W])
        uv = [sb(f"uv{i}", [128, 2 * D]) for i in range(2)]
        uvrest = [sb(f"uvrest{i}", [128, 2 * D]) for i in range(2)]
        parts = sb("parts", [128, SLOTS_PER_GROUP, 3, 2 * D], bf16)
        ustack = sb("ustack", [96, SLOTS_PER_GROUP, BLOCKS, D], bf16)
        m = {k: sb(f"m{k}", [128, 4, D]) for k in (1, 2)}
        mparts = [sb(f"mparts{i}", [128, 3, 4, D], bf16) for i in range(2)]
        mrest = sb("mrest", [128, 4, D])
        sT = [sb(f"sT{i}", [128, 128]) for i in range(2)]
        hT = sb("hT", [128, GROUP, 128])
        hsum = sb("hsum", [128, GROUP, 128])
        yT = [sb(f"yT{i}", [128, 128]) for i in range(2)]
        yp = [sb(f"yp{i}", [128, 128]) for i in range(2)]
        y = sb("y", [128, GROUP, D])
        stats = sb("stats", [128, GROUP, 6])
        meanvar = sb("meanvar", [128, GROUP, 2])
        varE = sb("varE", [128, GROUP])
        rstd = sb("rstd", [128, GROUP])
        root, inv, quot, twice, half = [sb(n, [128, GROUP]) for n in "root inv quot twice half".split()]
        outs = sb("outs", [128, GROUP, D])

        Z = [ctx.enter_context(nc.psum_tensor(f"Z{i}", [128, 4, D], f32)) for i in range(3)]
        PS = ctx.enter_context(nc.psum_tensor("PS", [128, 4, 128], f32))
        PU = ctx.enter_context(nc.psum_tensor("PU", [128, 512], f32))
        PM = ctx.enter_context(nc.psum_tensor("PM", [128, 512], f32))
        PA = ctx.enter_context(nc.psum_tensor("PA", [128, GROUP, 128], f32))
        PB = ctx.enter_context(nc.psum_tensor("PB", [128, GROUP, 128], f32))

        const_in, w_in, loaded, outs_free = map(sem, ["const_in", "w_in", "loaded", "outs_free"])
        stacked = [sem(f"stacked{s}") for s in range(SLOTS_PER_GROUP)]
        spilled = [sem(f"spilled{s}") for s in range(SLOTS_PER_GROUP)]
        bounce = [nc.dram_tensor(f"bounce{s}", (NODES * 3, D), bf16, kind="Internal").ap()
                  for s in range(SLOTS_PER_GROUP)]
        (wT_done, key_done, permT_done, adj1_done, adj2_done, rank_done, rowsum_done, xT_done, value_done, uv_done,
         z_done, sum_done, msg_done, yp_done, y_done) = [sem(f"pe_{s}") for s in (
            "wT key permT adj1 adj2 rank rowsum xT value uv z sum msg yp y".split())]
        (deg_ok, key_ok, diag_ok, above_ok, place_ok, perm_ok, nz_ok, adjrest_ok, adjlo_ok, rank_ok, over_ok, base_ok,
         take_ok, W_ok, mrest_ok, sT_ok, uvsum_ok, hT_ok, hsum_ok, stats_ok, mv_ok, varE_ok, outs_ok,
         inv_ok, quot_ok, twice_ok, half_ok, rstd_ok) = [sem(f"dve_{s}") for s in (
            "deg key diag above place perm nz adjrest adjlo rank over base take W mrest sT uvsum hT hsum "
            "stats mv varE outs inv quot twice half rstd".split())]
        uvrest_ok, uvlo_ok, mlo_ok = sem("pool_uvrest"), sem("pool_uvlo"), sem("pool_mlo")
        (wT_ok, permT_ok, adj1_ok, adj2_ok, adjhi_ok, adjmid_ok, rowsum_ok, xT_ok, uvhi_ok, uvmid_ok, m_ok, mhi_ok, mmid_ok,
         yp_ok, y_ok, root_ok, table_ok) = [sem(f"act_{s}") for s in (
            "wT permT adj1 adj2 adjhi adjmid rowsum xT uvhi uvmid m mhi mmid yp y root table".split())]

        spread = sb("spread", [128, 4, D])
        pairs = sb("pairs", [128, 4, D])
        messages = sb("messages", [128, 4, D])
        uvg = sb("uvg", [128, 2 * D])
        baseg = sb("baseg", [128, 128])
        onesf = sb("onesf", [128, 128])
        overs = sb("overs", [128, 1])
        some = sb("some", [128, 1], bf16)
        flag = sb("flag", [128, 1], mybir.dt.int32)
        (overs_ok, some_ok, count_done, flag_ok) = [sem(s) for s in "dve_overs dve_some pe_count dve_flag".split()]
        (g_loaded, g_turned, g_turned_ok, g_uv, g_uv_ok, g_spread_ok, g_rows, g_pairs_ok, g_messages_ok, g_sum, g_sT_ok,
         g_base_ok, g_msg, g_h_ok, g_back, g_y_ok, g_stats_ok, g_mv_ok, g_var_ok, g_root_ok, g_out_ok, g_stored,
         onesf_ok) = [sem(f"general_{s}") for s in (
            "loaded turned turned_ok uv uv_ok spread_ok rows pairs_ok messages_ok sum sT_ok base_ok msg h_ok back y_ok "
            "stats_ok mv_ok var_ok root_ok out_ok stored ones".split())]
        STEPS = NODES // 4

        def overflow(eng):
            eng.wait_ge(flag_ok, 1)
            return eng.value_load(flag[0:1, 0:1], min_val=0, max_val=128)

        x_v = x.rearrange("b n d -> n b d")
        adj_v = adj.rearrange("b n j -> n b j")
        out_v = out.rearrange("b n d -> n b d")
        block = ctx.enter_context(nc.Block())

        @block.sync
        def _(sp):
            def start_of(g):
                return g * GROUP if isinstance(g, int) else sp.snap(g * GROUP)

            def load(g, at):
                sp.wait_ge(adj1_done, g)
                sp.wait_ge(xT_done, g)
                sp.dma_start(adj_in[:, :, :], adj_v[:, bass.ds(at, GROUP), :]).then_inc(loaded, 16)
                sp.dma_start(x_in[:, :, :], x_v[:, bass.ds(at, GROUP), :]).then_inc(loaded, 16)

            def stack(g, s):
                k = g * SLOTS_PER_GROUP + s
                sp.wait_ge(uvlo_ok, k + 1)
                sp.wait_ge(uvhi_ok, k + 1)
                sp.wait_ge(uvmid_ok, k + 1)
                sp.dma_start(bounce[s].rearrange("(i p) d -> i p d", p=3), parts[:, s, :, 0:D]).then_inc(spilled[s], 16)
                sp.wait_ge(spilled[s], 16 * (g + 1))
                sp.dma_start(ustack[:, s, :, :], bounce[s].rearrange("(b k) d -> k b d", b=BLOCKS)).then_inc(stacked[s], 16)

            def store(g, at):
                sp.wait_ge(outs_ok, g + 1)
                sp.dma_start(out_v[:, bass.ds(at, GROUP), :], outs[:, :, :]).then_inc(outs_free, 16)

            def group(g, first=False, last=False, load_next=True):
                before = 0 if first else start_of(g - 1)
                after = start_of(g + 2)
                for q in range(GROUP):
                    stack(g, GROUP + q)
                    if q == 1 and not first:
                        store(g - 1, before)
                if load_next:
                    load(g + 2, after)
                if not last:
                    for q in range(GROUP):
                        stack(g + 1, q)

            sp.dma_start(CF[:, :], cf[:, :]).then_inc(const_in, 16)
            sp.dma_start(CB[:, :].bitcast(u16), cb[:, :]).then_inc(const_in, 16)
            load(0, 0)
            sp.dma_start(w1_in[:, :, :], w1.rearrange("l o c -> o l c")).then_inc(w_in, 16)
            sp.dma_start(w2_in[:, :, :], w2.rearrange("l o c -> o l c")).then_inc(w_in, 16)
            sp.dma_start(b1row[:, :, :], b1.rearrange("(a l) d -> a l d", a=1).broadcast_to((128, LAYERS, D)))\
              .then_inc(w_in, 16)
            sp.dma_start(b2col[:, :], b2.rearrange("l d -> d l"), allow_slow_non_contiguous=True).then_inc(w_in, 16)
            load(1, GROUP)
            for q in range(GROUP):
                stack(0, q)
            group(0, first=True)
            with sp.Fori(1, GROUPS - 2) as g:
                group(g)
            group(GROUPS - 2, load_next=False)
            group(GROUPS - 1, last=True, load_next=False)
            store(GROUPS - 1, GRAPHS - GROUP)
            sp.wait_ge(outs_free, 16 * (GROUPS + 1))

            def general(b):
                at = sp.snap(b)
                sp.dma_start(adj_in[:, 0, :], adj_v[:, bass.ds(at, 1), :].rearrange("n b j -> n (b j)")).then_inc(g_loaded, 16)
                sp.dma_start(x_in[:, 0, :], x_v[:, bass.ds(at, 1), :].rearrange("n b d -> n (b d)")).then_inc(g_loaded, 16)
                sp.wait_ge(g_out_ok, b + 1)
                sp.dma_start(out_v[:, bass.ds(at, 1), :].rearrange("n b d -> n (b d)"), outs[:, 0, :]).then_inc(g_stored, 16)

            with sp.If(overflow(sp) > 0):
                with sp.Fori(0, GRAPHS) as b:
                    general(b)
                sp.wait_ge(g_stored, 16 * (GRAPHS + 1))

        @block.tensor
        def _(pe):
            mm = nc.tensor.matmul

            def z_unit(g, n):
                s, k = divmod(n, QUADS)
                q = s % GROUP
                if k == 0:
                    pe.wait_ge(uvlo_ok, g * SLOTS_PER_GROUP + s + 1)
                    pe.wait_ge(uvhi_ok, g * SLOTS_PER_GROUP + s + 1)
                    pe.wait_ge(uvmid_ok, g * SLOTS_PER_GROUP + s + 1)
                    pe.wait_ge(stacked[s], 16 * (g + 1))
                    if s < GROUP:
                        pe.wait_ge(take_ok, g * GROUP + q + 1)
                if s or not isinstance(g, int) or g:
                    if k == 0:
                        pe.wait_ge(mrest_ok, g * SLOTS_PER_GROUP + s)
                    else:
                        pe.wait_ge(m_ok, 2 * (g * SLOTS_PER_GROUP + s - 1) + k)
                for t in range(4 * k, min(4 * k + 4, TILES)):
                    o = Z[k][:, t % 4, :]
                    lhs = take[:, q, 128 * t:128 * t + 128]
                    for p in range(3):
                        mm(o, lhs, parts[:, s, p, D:2 * D], start=(p == 0), stop=False)
                    mine = [i for i, (tt, _) in enumerate(PAIRS) if tt == t]
                    for i in mine:
                        last = mm(o, pick[0:96, i, :], ustack[:, s, PAIRS[i][1], :], start=False, stop=(i == mine[-1]))
                last.then_inc(z_done, 1)

            def sum_unit(g, s, k):
                q = s % GROUP
                if k == 1:
                    pe.wait_ge(W_ok, g * GROUP + q + 1)
                    pe.wait_ge(sT_ok, g * SLOTS_PER_GROUP + s)
                pe.wait_ge(m_ok, 2 * (g * SLOTS_PER_GROUP + s) + k)
                for t in range(4 * k, min(4 * k + 4, TILES)):
                    lo, hi = WINDOWS[t]
                    last = mm(PS[:, 0, lo:hi], m[k][:, t % 4, :], W[:, q, WOFF[t] - WOFF[SPLIT]:WOFF[t + 1] - WOFF[SPLIT]],
                              start=(t == SPLIT), stop=False, skip_group_check=True)
                last.then_inc(sum_done, 1)

            def sum_parts(g, s):
                q = s % GROUP
                pe.wait_ge(mlo_ok, g * SLOTS_PER_GROUP + s + 1)
                pe.wait_ge(mhi_ok, g * SLOTS_PER_GROUP + s + 1)
                pe.wait_ge(mmid_ok, g * SLOTS_PER_GROUP + s + 1)
                for t in range(SPLIT):
                    lo, hi = WINDOWS[t]
                    values = Wparts[:, q, 3 * WOFF[t]:3 * WOFF[t + 1]].rearrange("p (v i) -> p v i", v=3)
                    for p in range(3):
                        last = mm(PS[:, 0:3, lo:hi], mparts[s % 2][:, p, t, :], values, start=False,
                                  stop=(t == SPLIT - 1 and p == 2), skip_group_check=True)
                last.then_inc(sum_done, 1)

            def msg(g, s):
                pe.wait_ge(sT_ok, g * SLOTS_PER_GROUP + s + 1)
                if 1 <= s <= GROUP:
                    pe.wait_ge(hT_ok, g * SLOTS_PER_GROUP + s)
                else:
                    pe.wait_ge(y_ok, g * GROUP + max(0, s - GROUP))
                mm(PM[:, 0:128], w2T[:, s // GROUP, :], sT[s % 2][:, :], start=True, stop=True).then_inc(msg_done, 1)

            def yp_step(g, q):
                pe.wait_ge(hT_ok, g * SLOTS_PER_GROUP + GROUP + q + 1)
                nc.tensor.transpose(PM[:, 0:128], yT[q % 2][:, :], ident).then_inc(yp_done, 1)

            def y_step(g, q):
                pe.wait_ge(yp_ok, g * GROUP + q + 1)
                if q == 0:
                    pe.wait_ge(permT_ok, g + 1)
                mm(PM[:, 0:128], permT[:, q, :], yp[q % 2][:, :], start=True, stop=True).then_inc(y_done, 1)

            def uv_step(g, s):
                k = g * SLOTS_PER_GROUP + s
                pe.wait_ge(uvsum_ok, k)
                if s < GROUP:
                    pe.wait_ge(xT_ok, g + 1)
                    h = xT
                else:
                    pe.wait_ge(hT_ok, k - GROUP + 1)
                    h = hT
                mm(PU[:, 0:2 * D], h[:, s % GROUP, :], w1T[:, s // GROUP, :], start=True, stop=True)\
                    .then_inc(uv_done, 1)

            def key_step(g):
                pe.wait_ge(diag_ok, g + 1)
                pe.wait_ge(W_ok, max(0, (g - 1) * GROUP + 3) if isinstance(g, int) else (g - 1) * GROUP + 3)
                o = PA[:, :, :].rearrange("p q i -> p (q i)")
                mm(o, onesb, degdiag[:, :, :].rearrange("p q i -> p (q i)"), start=True, stop=False)
                mm(o, onesb, tiediag, start=False, stop=True).then_inc(key_done, 1)

            def permT_step(g):
                pe.wait_ge(perm_ok, g + 1)
                pe.wait_ge(W_ok, g * GROUP + 2)
                for q in range(GROUP):
                    last = nc.tensor.transpose(PB[:, q, :], perm[:, q, :], ident)
                last.then_inc(permT_done, 1)

            def adj1_step(g):
                pe.wait_ge(perm_ok, g + 1)
                pe.wait_ge(above_ok, g + 1)
                for q in range(GROUP):
                    last = mm(PA[:, q, :], adj_in[:, q, :], perm[:, q, :], start=True, stop=True)
                last.then_inc(adj1_done, 1)

            def adj2_step(g):
                pe.wait_ge(adj1_ok, g + 1)
                for q in range(GROUP):
                    last = mm(PA[:, q, :], perm[:, q, :], adj1[:, q, :], start=True, stop=True)
                last.then_inc(adj2_done, 1)

            def rank_step(g):
                pe.wait_ge(nz_ok, g + 1)
                pe.wait_ge(xT_ok, g + 1)
                mm(PB[:, :, :].rearrange("p q i -> p (q i)"), upto, nz[:, :, :].rearrange("p q i -> p (q i)"),
                   start=True, stop=True).then_inc(rank_done, 1)

            def rowsum_step(g):
                pe.wait_ge(adjlo_ok, g + 1)
                pe.wait_ge(adjhi_ok, g + 1)
                pe.wait_ge(adjmid_ok, g + 1)
                pe.wait_ge(adj2_ok, g + 1)
                for p in range(3):
                    last = mm(PA[:, :, :].rearrange("p q i -> p (q i)"), onesb,
                              adjp[:, p, :, :].rearrange("p q i -> p (q i)"), start=(p == 0), stop=(p == 2))
                last.then_inc(rowsum_done, 1)

            def xT_step(g):
                pe.wait_ge(perm_ok, g + 1)
                pe.wait_ge(W_ok, g * GROUP)
                for q in range(GROUP):
                    last = mm(PB[:, q, :], x_in[:, q, :], perm[:, q, :], start=True, stop=True)
                last.then_inc(xT_done, 1)

            def value_step(g, q):
                pe.wait_ge(take_ok, g * GROUP + q + 1)
                if q == 0:
                    pe.wait_ge(rowsum_ok, g + 1)
                elif q == 1:
                    pe.wait_ge(over_ok, g + 1)
                else:
                    pe.wait_ge(W_ok, g * GROUP + q - 1)
                if q == 3:
                    pe.wait_ge(permT_ok, g + 1)
                bank = (PA, PB)[q % 2][:, :, :].rearrange("p q i -> p (q i)")
                for t, (lo, hi) in enumerate(WINDOWS):
                    lhs = take[:, q, 128 * t:128 * t + 128]
                    if t < SPLIT:
                        o = bank[:, 3 * WOFF[t]:3 * WOFF[t + 1]].rearrange("p (v i) -> p v i", v=3)
                        mm(o, lhs, adjp[:, 0:3, q, lo:hi], start=True, stop=True)
                    else:
                        at = SPLIT_W - WOFF[SPLIT]
                        for p in range(3):
                            last = mm(bank[:, at + WOFF[t]:at + WOFF[t + 1]], lhs, adjp[:, p, q, lo:hi],
                                      start=(p == 0), stop=(p == 2))
                last.then_inc(value_done, 1)

            def group(g, first=False, last=False):
                for n in range(UNITS):
                    z_unit(g, n)
                    if n % QUADS == 2:
                        sum_unit(g, n // QUADS, 1)
                    if n % QUADS == 0 and n:
                        sum_unit(g, n // QUADS - 1, 2)
                        sum_parts(g, n // QUADS - 1)
                    if n == 0 and not first:
                        sum_unit(g - 1, SLOTS_PER_GROUP - 1, 2)
                        sum_parts(g - 1, SLOTS_PER_GROUP - 1)
                    if n == 0 and not first: y_step(g - 1, 2)
                    if n == 1 and not first: msg(g - 1, 7)
                    if n == 1: value_step(g, 2)
                    if n == 2 and not first: yp_step(g - 1, 3)
                    if n == 2: uv_step(g, 3)
                    if n == 2: permT_step(g)
                    if n == 3 and not first: y_step(g - 1, 3)
                    if n == 3 and not last: key_step(g + 1)
                    if n == 4: msg(g, 0)
                    if n == 5: uv_step(g, 4)
                    if n == 5: value_step(g, 3)
                    if n == 7: msg(g, 1)
                    if n == 7 and not last: adj1_step(g + 1)
                    if n == 7 and not last: xT_step(g + 1)
                    if n == 8: uv_step(g, 5)
                    if n == 10: msg(g, 2)
                    if n == 10 and not last: adj2_step(g + 1)
                    if n == 11: uv_step(g, 6)
                    if n == 13: msg(g, 3)
                    if n == 14: uv_step(g, 7)
                    if n == 14 and not last: rank_step(g + 1)
                    if n == 16: msg(g, 4)
                    if n == 16 and not last: rowsum_step(g + 1)
                    if n == 17: yp_step(g, 0)
                    if n == 17 and not last: uv_step(g + 1, 0)
                    if n == 18: y_step(g, 0)
                    if n == 19: msg(g, 5)
                    if n == 19 and not last: value_step(g + 1, 0)
                    if n == 20: yp_step(g, 1)
                    if n == 20 and not last: uv_step(g + 1, 1)
                    if n == 21: y_step(g, 1)
                    if n == 22: msg(g, 6)
                    if n == 22 and not last: value_step(g + 1, 1)
                    if n == 23: yp_step(g, 2)
                    if n == 23 and not last: uv_step(g + 1, 2)
                    if n == 8 and last:
                        pe.wait_ge(some_ok, 1)
                        pe.wait_ge(W_ok, g * GROUP + 3)
                        mm(PA[:, 0, 0:1], onesb, some[:, :], start=True, stop=True).then_inc(count_done, 1)

            pe.wait_ge(const_in, 32)
            pe.wait_ge(w_in, 64)
            for l in range(LAYERS):
                nc.tensor.transpose(PA[:, 2 * l, :], w1_in[:, l, 0:D], ident)
                nc.tensor.transpose(PA[:, 2 * l + 1, :], w1_in[:, l, D:2 * D], ident)
            for l in range(LAYERS):
                last = nc.tensor.transpose(PB[:, l, :], w2_in[:, l, :], ident)
            last.then_inc(wT_done, 1)
            pe.wait_ge(wT_ok, 2)
            key_step(0)
            adj1_step(0)
            xT_step(0)
            adj2_step(0)
            rank_step(0)
            rowsum_step(0)
            uv_step(0, 0)
            uv_step(0, 1)
            value_step(0, 0)
            uv_step(0, 2)
            value_step(0, 1)
            group(0, first=True)
            with pe.Fori(1, GROUPS - 1) as g:
                group(g)
            group(GROUPS - 1, last=True)
            g = GROUPS - 1
            sum_unit(g, SLOTS_PER_GROUP - 1, 2)
            sum_parts(g, SLOTS_PER_GROUP - 1)
            y_step(g, 2)
            msg(g, 7)
            yp_step(g, 3)
            y_step(g, 3)

            def general(b):
                pe.wait_ge(g_loaded, 32 * (b + 1))
                nc.tensor.transpose(PA[:, 0, :], adj_in[:, 0, :], ident)
                nc.tensor.transpose(PA[:, 1, :], x_in[:, 0, :], ident).then_inc(g_turned, 1)
                pe.wait_ge(g_turned_ok, 2 * b + 1)
                mm(PA[:, 2, :], onesf[:, :], adj1[:, 0, :], start=True, stop=True).then_inc(g_turned, 1)
                for l in range(LAYERS):
                    h = (xT, hT)[l]
                    if l == 0:
                        pe.wait_ge(g_turned_ok, 2 * b + 2)
                    else:
                        pe.wait_ge(g_h_ok, 2 * b + 1)
                    mm(PU[:, 0:2 * D], h[:, 0, :], w1T[:, l, :], start=True, stop=True).then_inc(g_uv, 1)
                    with pe.Fori(0, STEPS) as i:
                        n = (b * LAYERS + l) * STEPS + i + 1
                        pe.wait_ge(g_spread_ok, n)
                        mm(Z[0][:, :, :].rearrange("p r d -> p (r d)"), onesf[:, :],
                           spread[:, :, :].rearrange("p r d -> p (r d)"), start=True, stop=True).then_inc(g_rows, 1)
                        pe.wait_ge(g_messages_ok, n)
                        for r in range(4):
                            last = mm(PS[:, 0, bass.ds(4 * i + r, 1)], messages[:, r, :], adj1[:, 0, bass.ds(4 * i + r, 1)],
                                      start=True, stop=True)
                        last.then_inc(g_sum, 1)
                    pe.wait_ge(g_sT_ok, 2 * b + l + 1)
                    mm(PM[:, 0:128], w2T[:, l, :], sT[0][:, :], start=True, stop=True).then_inc(g_msg, 1)
                pe.wait_ge(g_h_ok, 2 * b + 2)
                nc.tensor.transpose(PM[:, 0:128], hT[:, 0, :], ident).then_inc(g_back, 1)

            with pe.If(overflow(pe) > 0):
                pe.wait_ge(onesf_ok, 1)
                with pe.Fori(0, GRAPHS) as b:
                    general(b)

        @block.scalar
        def _(act):
            def copy(o, i):
                return nc.scalar.activation(o, i, ACT.Copy)

            def relu_unit(g, n):
                s, k = divmod(n, QUADS)
                slot = g * SLOTS_PER_GROUP + s
                act.wait_ge(z_done, g * UNITS + n + 1)
                if k == 0:
                    if s >= 2 or not isinstance(g, int) or g:
                        act.wait_ge(sum_done, QUADS * (slot - 1))
                    nc.scalar.activation(mparts[s % 2][:, 0, :, :], Z[0][:, :, :], ACT.Relu).then_inc(mhi_ok, 1)
                else:
                    if s or not isinstance(g, int) or g:
                        act.wait_ge(sum_done, QUADS * (slot - 1) + k)
                    tiles = min(4, TILES - 4 * k)
                    nc.scalar.activation(m[k][:, 0:tiles, :], Z[k][:, 0:tiles, :], ACT.Relu).then_inc(m_ok, 1)

            def mmid_step(g, s):
                act.wait_ge(mrest_ok, g * SLOTS_PER_GROUP + s + 1)
                copy(mparts[s % 2][:, 1, :, :], mrest[:, :, :]).then_inc(mmid_ok, 1)

            def yp_copy(g, q):
                act.wait_ge(yp_done, g * GROUP + q + 1)
                if q >= 2 or not isinstance(g, int) or g:
                    act.wait_ge(y_done, g * GROUP + q - 1)
                copy(yp[q % 2][:, :], PM[:, 0:128]).then_inc(yp_ok, 1)

            def y_copy(g, q):
                act.wait_ge(y_done, g * GROUP + q + 1)
                if q == 0:
                    act.wait_ge(outs_ok, g)
                copy(y[:, q, :], PM[:, 0:128]).then_inc(y_ok, 1)

            def hi_step(g, s):
                k = g * SLOTS_PER_GROUP + s
                act.wait_ge(uvsum_ok, k + 1)
                if not isinstance(g, int) or g:
                    act.wait_ge(z_done, (g - 1) * UNITS + (s + 1) * QUADS)
                    act.wait_ge(stacked[s], 16 * g)
                copy(parts[:, s, 0, :], uv[s % 2][:, :]).then_inc(uvhi_ok, 1)

            def mid_step(g, s):
                act.wait_ge(uvrest_ok, g * SLOTS_PER_GROUP + s + 1)
                copy(parts[:, s, 1, :], uvrest[s % 2][:, :]).then_inc(uvmid_ok, 1)

            def permT_copy(g):
                act.wait_ge(permT_done, g + 1)
                act.wait_ge(y_done, g * GROUP)
                copy(permT[:, :, :], PB[:, :, :]).then_inc(permT_ok, 1)

            def adj1_copy(g):
                act.wait_ge(adj1_done, g + 1)
                act.wait_ge(adj2_done, g)
                copy(adj1[:, :, :], PA[:, :, :]).then_inc(adj1_ok, 1)

            def adj2_copy(g):
                act.wait_ge(adj2_done, g + 1)
                act.wait_ge(nz_ok, g)
                act.wait_ge(adjrest_ok, g)
                copy(adj2[:, :, :], PA[:, :, :]).then_inc(adj2_ok, 1)

            def adjhi_step(g):
                act.wait_ge(adj2_ok, g + 1)
                act.wait_ge(value_done, g * GROUP)
                act.wait_ge(rowsum_done, g)
                copy(adjp[:, 0, :, :], adj2[:, :, :]).then_inc(adjhi_ok, 1)

            def adjmid_step(g):
                act.wait_ge(adjrest_ok, g + 1)
                copy(adjp[:, 1, :, :], adjrest[:, :, :]).then_inc(adjmid_ok, 1)

            def rowsum_copy(g):
                act.wait_ge(rowsum_done, g + 1)
                act.wait_ge(base_ok, 2 * g)
                copy(rowsum[:, :, :], PA[:, :, :]).then_inc(rowsum_ok, 1)

            def xT_copy(g):
                act.wait_ge(xT_done, g + 1)
                act.wait_ge(base_ok, 2 * g)
                if not isinstance(g, int) or g:
                    act.wait_ge(uv_done, (g - 1) * SLOTS_PER_GROUP + GROUP)
                copy(xT[:, :, :], PB[:, :, :]).then_inc(xT_ok, 1)

            def root_step(g):
                act.wait_ge(varE_ok, g + 1)
                nc.scalar.activation(root[:, :], varE[:, :], ACT.Sqrt).then_inc(root_ok, 1)

            def group(g, first=False, last=False):
                for n in range(UNITS):
                    relu_unit(g, n)
                    if n % QUADS == 1: mmid_step(g, n // QUADS)
                    if n == 0: hi_step(g, 2)
                    if n == 0 and not first: y_copy(g - 1, 2)
                    if n == 1: mid_step(g, 2)
                    if n == 2 and not first: yp_copy(g - 1, 3)
                    if n == 3: hi_step(g, 3)
                    if n == 3 and not first: y_copy(g - 1, 3)
                    if n == 3: permT_copy(g)
                    if n == 4: mid_step(g, 3)
                    if n == 6: hi_step(g, 4)
                    if n == 7: mid_step(g, 4)
                    if n == 8 and not last: adj1_copy(g + 1)
                    if n == 8 and not last: xT_copy(g + 1)
                    if n == 9: hi_step(g, 5)
                    if n == 9 and not first: root_step(g - 1)
                    if n == 10: mid_step(g, 5)
                    if n == 11 and not last: adj2_copy(g + 1)
                    if n == 11 and not last: adjhi_step(g + 1)
                    if n == 12: hi_step(g, 6)
                    if n == 13: mid_step(g, 6)
                    if n == 14 and not last: adjmid_step(g + 1)
                    if n == 15: hi_step(g, 7)
                    if n == 16: mid_step(g, 7)
                    if n == 17: yp_copy(g, 0)
                    if n == 17 and not last: rowsum_copy(g + 1)
                    if n == 18 and not last: hi_step(g + 1, 0)
                    if n == 18: y_copy(g, 0)
                    if n == 19 and not last: mid_step(g + 1, 0)
                    if n == 20: yp_copy(g, 1)
                    if n == 21 and not last: hi_step(g + 1, 1)
                    if n == 21: y_copy(g, 1)
                    if n == 22 and not last: mid_step(g + 1, 1)
                    if n == 23: yp_copy(g, 2)

            act.wait_ge(const_in, 32)
            nc.scalar.activation(root[:, 0:1], iota[:, 0:1], ACT.Sqrt).then_inc(table_ok, 1)
            act.wait_ge(table_ok, 1)
            act.wait_ge(wT_done, 1)
            copy(w1T[:, :, :].rearrange("p l o -> p (l o)"), PA[:, :, :].rearrange("p q i -> p (q i)"))\
                .then_inc(wT_ok, 1)
            copy(w2T[:, :, :], PB[:, 0:2, :]).then_inc(wT_ok, 1)
            adj1_copy(0)
            xT_copy(0)
            adj2_copy(0)
            adjhi_step(0)
            adjmid_step(0)
            rowsum_copy(0)
            for q in range(2):
                hi_step(0, q)
                mid_step(0, q)
            group(0, first=True)
            with act.Fori(1, GROUPS - 1) as g:
                group(g)
            group(GROUPS - 1, last=True)
            g = GROUPS - 1
            y_copy(g, 2)
            yp_copy(g, 3)
            y_copy(g, 3)
            root_step(g)

            def general(b):
                act.wait_ge(g_turned, 2 * b + 1)
                copy(adj1[:, 0, :], PA[:, 0, :]).then_inc(g_turned_ok, 1)
                act.wait_ge(g_turned, 2 * b + 2)
                copy(xT[:, 0, :], PA[:, 1, :])
                copy(rowsum[:, 0, :], PA[:, 2, :]).then_inc(g_turned_ok, 1)
                for l in range(LAYERS):
                    with act.Fori(0, STEPS) as i:
                        act.wait_ge(g_pairs_ok, (b * LAYERS + l) * STEPS + i + 1)
                        nc.scalar.activation(messages[:, :, :], pairs[:, :, :], ACT.Relu).then_inc(g_messages_ok, 1)
                    act.wait_ge(g_sum, (b * LAYERS + l + 1) * STEPS)
                    copy(sT[0][:, :], PS[:, 0, :]).then_inc(g_sT_ok, 1)
                act.wait_ge(g_back, b + 1)
                copy(y[:, 0, :], PM[:, 0:128]).then_inc(g_y_ok, 1)
                act.wait_ge(g_var_ok, b + 1)
                nc.scalar.activation(root[:, 0:1], varE[:, 0:1], ACT.Sqrt).then_inc(g_root_ok, 1)

            with act.If(overflow(act) > 0):
                with act.Fori(0, GRAPHS) as b:
                    general(b)

        @block.gpsimd
        def _(pool):
            def mlo_step(g, s):
                k = g * SLOTS_PER_GROUP + s
                pool.wait_ge(mmid_ok, k + 1)
                pool.wait_ge(mrest_ok, k + 1)
                nc.gpsimd.tensor_tensor(mparts[s % 2][:, 2, :, :], mrest[:, :, :], mparts[s % 2][:, 1, :, :], ALU.subtract)\
                    .then_inc(mlo_ok, 1)

            def rest_step(g, s):
                k = g * SLOTS_PER_GROUP + s
                pool.wait_ge(uvhi_ok, k + 1)
                if s >= 2 or not isinstance(g, int) or g:
                    pool.wait_ge(uvmid_ok, k - 1)
                nc.gpsimd.tensor_tensor(uvrest[s % 2][:, :], uv[s % 2][:, :], parts[:, s, 0, :], ALU.subtract)\
                    .then_inc(uvrest_ok, 1)

            def lo_step(g, s):
                k = g * SLOTS_PER_GROUP + s
                pool.wait_ge(uvmid_ok, k + 1)
                pool.wait_ge(uvrest_ok, k + 1)
                nc.gpsimd.tensor_tensor(parts[:, s, 2, :], uvrest[s % 2][:, :], parts[:, s, 1, :], ALU.subtract)\
                    .then_inc(uvlo_ok, 1)

            def group(g, first=False, last=False):
                for n in range(UNITS):
                    if n == 0: rest_step(g, 2)
                    if n == 1: mlo_step(g, 0)
                    if n == 1: lo_step(g, 2)
                    if n == 3: rest_step(g, 3)
                    if n == 4: mlo_step(g, 1)
                    if n == 4: lo_step(g, 3)
                    if n == 6: rest_step(g, 4)
                    if n == 7: mlo_step(g, 2)
                    if n == 7: lo_step(g, 4)
                    if n == 9: rest_step(g, 5)
                    if n == 10: mlo_step(g, 3)
                    if n == 10: lo_step(g, 5)
                    if n == 12: rest_step(g, 6)
                    if n == 13: mlo_step(g, 4)
                    if n == 13: lo_step(g, 6)
                    if n == 15: rest_step(g, 7)
                    if n == 16: mlo_step(g, 5)
                    if n == 16: lo_step(g, 7)
                    if n == 18 and not last: rest_step(g + 1, 0)
                    if n == 19: mlo_step(g, 6)
                    if n == 19 and not last: lo_step(g + 1, 0)
                    if n == 21 and not last: rest_step(g + 1, 1)
                    if n == 22: mlo_step(g, 7)
                    if n == 22 and not last: lo_step(g + 1, 1)

            for s in range(2):
                rest_step(0, s)
                lo_step(0, s)
            group(0, first=True)
            with pool.Fori(1, GROUPS - 1) as g:
                group(g)
            group(GROUPS - 1, last=True)

        @block.vector
        def _(dve):
            V = nc.vector

            def wide(a):
                return a.rearrange("p (q i) -> p q i", q=1).broadcast_to((128, GROUP, 128))

            def col(a):
                return a[:, :].rearrange("p (q i) -> p q i", i=1).broadcast_to((128, GROUP, 128))

            def deg_step(g):
                dve.wait_ge(loaded, 32 * (g + 1))
                for q in range(GROUP):
                    last = V.tensor_scalar(junk[:, q, :], adj_in[:, q, :], 0.0, None, ALU.not_equal, ALU.add,
                                           accum_out=deg[:, q:q + 1])
                last.then_inc(deg_ok, 1)
                dve.wait_ge(deg_ok, g + 1)
                V.tensor_scalar(key[:, :], deg[:, :], tie, None, ALU.add).then_inc(key_ok, 1)
                dve.wait_ge(key_done, g)
                V.tensor_tensor(degdiag[:, :, :], wide(identb), col(deg), ALU.mult).then_inc(diag_ok, 1)

            def place_step(g):
                dve.wait_ge(key_done, g + 1)
                dve.wait_ge(key_ok, g + 1)
                V.tensor_tensor(above[:, :, :], PA[:, :, :], col(key), ALU.is_gt).then_inc(above_ok, 1)
                dve.wait_ge(above_ok, g + 1)
                V.tensor_reduce(place[:, :], above[:, :, :], AX.X, ALU.add).then_inc(place_ok, 1)

            def perm_step(g):
                dve.wait_ge(place_ok, g + 1)
                dve.wait_ge(permT_done, g)
                dve.wait_ge(xT_done, g)
                V.tensor_tensor(perm[:, :, :], wide(iota), col(place), ALU.is_equal).then_inc(perm_ok, 1)

            def adj_step(g):
                dve.wait_ge(adj2_ok, g + 1)
                dve.wait_ge(rank_done, g)
                V.tensor_scalar(nz[:, :, :], adj2[:, :, :], 0.0, None, ALU.not_equal).then_inc(nz_ok, 1)
                dve.wait_ge(adjhi_ok, g + 1)
                dve.wait_ge(adjmid_ok, g)
                V.tensor_tensor(adjrest[:, :, :], adj2[:, :, :], adjp[:, 0, :, :], ALU.subtract)\
                    .then_inc(adjrest_ok, 1)

            def adjlo_step(g):
                dve.wait_ge(adjmid_ok, g + 1)
                V.tensor_tensor(adjp[:, 2, :, :], adjrest[:, :, :], adjp[:, 1, :, :], ALU.subtract)\
                    .then_inc(adjlo_ok, 1)

            def rank_step(g):
                dve.wait_ge(rank_done, g + 1)
                V.tensor_tensor(rank[:, :, :], PB[:, :, :], nz[:, :, :], ALU.mult).then_inc(rank_ok, 1)
                V.scalar_tensor_tensor(out=junk[:, :, :], in0=PB[:, :, :], scalar=0.0, in1=wide(caps),
                                       op0=ALU.add, op1=ALU.is_gt, accum_out=over[:, bass.ds(g, 1)])\
                    .then_inc(over_ok, 1)

            def base_step(g):
                dve.wait_ge(rowsum_ok, g + 1)
                dve.wait_ge(xT_ok, g + 1)
                dve.wait_ge(hsum_ok, g * GROUP)
                V.scalar_tensor_tensor(out=base0[:, :, :], in0=rowsum[:, :, :], scalar=b2col[:, 0:1],
                                       in1=xT[:, :, :], op0=ALU.mult, op1=ALU.add).then_inc(base_ok, 1)
                V.scalar_tensor_tensor(out=base1[:, :, :], in0=rowsum[:, :, :], scalar=b2col[:, 1:2],
                                       in1=xT[:, :, :], op0=ALU.mult, op1=ALU.add).then_inc(base_ok, 1)

            def take_step(g, q):
                dve.wait_ge(rank_ok, g + 1)
                if not isinstance(g, int) or g:
                    dve.wait_ge(z_done, (g - 1) * UNITS + (GROUP + q + 1) * QUADS)
                r0 = off = 0
                for rows, cap in REGIONS:
                    n = rows * cap
                    o = take[:, q, off:off + n].rearrange("p (k i) -> p k i", i=rows)
                    c = rankc[:, off:off + n].rearrange("p (k i) -> p k i", i=rows)
                    r = rank[:, q, r0:r0 + rows].rearrange("p (k i) -> p k i", k=1).broadcast_to((128, cap, rows))
                    last = V.tensor_tensor(o, r, c, ALU.is_equal)
                    r0, off = r0 + rows, off + n
                last.then_inc(take_ok, 1)

            def W_step(g, q):
                dve.wait_ge(value_done, g * GROUP + q + 1)
                if not isinstance(g, int) or g:
                    dve.wait_ge(sum_done, (g - 1) * UNITS + (GROUP + q + 1) * QUADS)
                bank = (PA, PB)[q % 2][:, :, :].rearrange("p q i -> p (q i)")
                V.tensor_tensor(Wparts[:, q, :], bank[:, 0:SPLIT_W], mask[:, 0:SPLIT_W], ALU.mult)
                V.tensor_tensor(W[:, q, :], bank[:, SPLIT_W:SPLIT_W + WHOLE_W], mask[:, SPLIT_W:SPLIT_W + WHOLE_W],
                                ALU.mult).then_inc(W_ok, 1)

            def mrest_step(g, s):
                k = g * SLOTS_PER_GROUP + s
                dve.wait_ge(mhi_ok, k + 1)
                dve.wait_ge(mlo_ok, k)
                dve.wait_ge(mmid_ok, k)
                V.scalar_tensor_tensor(out=mrest[:, :, :], in0=Z[0][:, :, :], scalar=0.0, in1=mparts[s % 2][:, 0, :, :],
                                       op0=ALU.max, op1=ALU.subtract).then_inc(mrest_ok, 1)

            def sT_step(g, s):
                k = g * SLOTS_PER_GROUP + s
                dve.wait_ge(sum_done, QUADS * (k + 1))
                if s >= 2 or not isinstance(g, int) or g:
                    dve.wait_ge(msg_done, k - 1)
                V.tensor_reduce(sT[s % 2][:, 0:SPLIT_ROWS], PS[:, 0:3, 0:SPLIT_ROWS].rearrange("p v i -> p i v"),
                                AX.X, ALU.add)
                V.tensor_copy(sT[s % 2][:, SPLIT_ROWS:128], PS[:, 0, SPLIT_ROWS:128]).then_inc(sT_ok, 1)

            def uv_step(g, s):
                k = g * SLOTS_PER_GROUP + s
                dve.wait_ge(uv_done, k + 1)
                if s >= 2 or not isinstance(g, int) or g:
                    dve.wait_ge(uvhi_ok, k - 1)
                    dve.wait_ge(uvrest_ok, k - 1)
                V.tensor_copy(uv[s % 2][:, D:2 * D], PU[:, D:2 * D])
                V.tensor_tensor(uv[s % 2][:, 0:D], PU[:, 0:D], b1row[:, s // GROUP, :], ALU.add)\
                    .then_inc(uvsum_ok, 1)

            def h_step(g, s):
                dve.wait_ge(msg_done, g * SLOTS_PER_GROUP + s + 1)
                q = s % GROUP
                if s < GROUP:
                    dve.wait_ge(base_ok, 2 * g + 1)
                    if q == 0:
                        dve.wait_ge(uv_done, g * SLOTS_PER_GROUP)
                    V.tensor_tensor(hT[:, q, :], PM[:, 0:128], base0[:, q, :], ALU.add).then_inc(hT_ok, 1)
                else:
                    dve.wait_ge(hsum_ok, g * GROUP + q + 1)
                    if q >= 2 or not isinstance(g, int) or g:
                        dve.wait_ge(yp_done, g * GROUP + q - 1)
                    V.tensor_tensor(yT[q % 2][:, :], PM[:, 0:128], hsum[:, q, :], ALU.add).then_inc(hT_ok, 1)

            def hsum_step(g, q):
                dve.wait_ge(hT_ok, g * SLOTS_PER_GROUP + q + 1)
                dve.wait_ge(base_ok, 2 * g + 2)
                V.tensor_tensor(hsum[:, q, :], hT[:, q, :], base1[:, q, :], ALU.add).then_inc(hsum_ok, 1)

            def norm_stats(g):
                dve.wait_ge(y_ok, (g + 1) * GROUP)
                for q in range(GROUP):
                    last = V.bn_stats(stats[:, q, :], y[:, q, :])
                last.then_inc(stats_ok, 1)
                dve.wait_ge(stats_ok, g + 1)
                V.memset(varE[:, :], 0.0)
                for q in range(GROUP):
                    last = V.bn_aggr(meanvar[:, q, :], stats[:, q, :])
                last.then_inc(mv_ok, 1)
                dve.wait_ge(mv_ok, g + 1)
                V.tensor_scalar(varE[:, :], meanvar[:, :, 1], EPS, None, ALU.add).then_inc(varE_ok, 1)

            def rstd_step(n, k):
                V.reciprocal(inv[:, 0:n], root[:, 0:n]).then_inc(inv_ok, 1)
                dve.wait_ge(inv_ok, k + 1)
                V.tensor_tensor(quot[:, 0:n], varE[:, 0:n], inv[:, 0:n], ALU.mult).then_inc(quot_ok, 1)
                dve.wait_ge(quot_ok, k + 1)
                V.tensor_tensor(twice[:, 0:n], quot[:, 0:n], root[:, 0:n], ALU.add).then_inc(twice_ok, 1)
                dve.wait_ge(twice_ok, k + 1)
                V.tensor_scalar(half[:, 0:n], twice[:, 0:n], 0.5, None, ALU.mult).then_inc(half_ok, 1)
                dve.wait_ge(half_ok, k + 1)
                V.reciprocal(rstd[:, 0:n], half[:, 0:n]).then_inc(rstd_ok, 1)
                dve.wait_ge(rstd_ok, k + 1)

            def norm_rstd(g):
                dve.wait_ge(root_ok, g + 1)
                rstd_step(GROUP, g)

            def norm_out(g):
                dve.wait_ge(outs_free, 16 * (g + 1))
                for q in range(GROUP):
                    last = V.tensor_scalar(outs[:, q, :], y[:, q, :], meanvar[:, q, 0:1], rstd[:, q:q + 1],
                                           ALU.subtract, ALU.mult)
                last.then_inc(outs_ok, 1)

            def group(g, first=False, last=False):
                for n in range(UNITS):
                    if n % QUADS == 0: mrest_step(g, n // QUADS)
                    if n == 0 and not first: sT_step(g - 1, SLOTS_PER_GROUP - 1)
                    if n % QUADS == 0 and n: sT_step(g, n // QUADS - 1)
                    if n == 0: W_step(g, 1)
                    if n == 1 and not first: h_step(g - 1, 7)
                    if n == 1 and not last: deg_step(g + 1)
                    if n == 2: uv_step(g, 3)
                    if n == 2: W_step(g, 2)
                    if n == 3: take_step(g, 3)
                    if n == 4: h_step(g, 0)
                    if n == 4 and not last: place_step(g + 1)
                    if n == 5: hsum_step(g, 0)
                    if n == 5: uv_step(g, 4)
                    if n == 5 and not last: perm_step(g + 1)
                    if n == 6: W_step(g, 3)
                    if n == 7: h_step(g, 1)
                    if n == 7 and not first: norm_stats(g - 1)
                    if n == 8: hsum_step(g, 1)
                    if n == 8: uv_step(g, 5)
                    if n == 10: h_step(g, 2)
                    if n == 10 and not first: norm_rstd(g - 1)
                    if n == 11: hsum_step(g, 2)
                    if n == 11: uv_step(g, 6)
                    if n == 11 and not first: norm_out(g - 1)
                    if n == 13: h_step(g, 3)
                    if n == 13 and not last: adj_step(g + 1)
                    if n == 14: hsum_step(g, 3)
                    if n == 14: uv_step(g, 7)
                    if n == 15 and not last: adjlo_step(g + 1)
                    if n == 16: h_step(g, 4)
                    if n == 16 and not last: rank_step(g + 1)
                    if n == 17 and not last: uv_step(g + 1, 0)
                    if n == 17 and not last: take_step(g + 1, 0)
                    if n == 19: h_step(g, 5)
                    if n == 19 and not last: base_step(g + 1)
                    if n == 20 and not last: uv_step(g + 1, 1)
                    if n == 20 and not last: take_step(g + 1, 1)
                    if n == 21 and not last: W_step(g + 1, 0)
                    if n == 22: h_step(g, 6)
                    if n == 23 and not last: uv_step(g + 1, 2)
                    if n == 23 and not last: take_step(g + 1, 2)
                    if n == 6 and last:
                        dve.wait_ge(over_ok, GROUPS)
                        V.tensor_reduce(overs[:, :], over[:, :], AX.X, ALU.add).then_inc(overs_ok, 1)
                        dve.wait_ge(overs_ok, 1)
                        V.tensor_scalar(some[:, :], overs[:, :], 1.0, None, ALU.min).then_inc(some_ok, 1)
                    if n == 9 and last:
                        dve.wait_ge(count_done, 1)
                        V.tensor_copy(flag[:, :], PA[:, 0, 0:1]).then_inc(flag_ok, 1)

            V.memset(outs[:, :, :], 0.0).then_inc(outs_free, 16)
            dve.wait_ge(const_in, 32)
            dve.wait_ge(w_in, 64)
            deg_step(0)
            place_step(0)
            perm_step(0)
            adj_step(0)
            adjlo_step(0)
            rank_step(0)
            take_step(0, 0)
            uv_step(0, 0)
            take_step(0, 1)
            uv_step(0, 1)
            base_step(0)
            W_step(0, 0)
            uv_step(0, 2)
            take_step(0, 2)
            group(0, first=True)
            with dve.Fori(1, GROUPS - 1) as g:
                group(g)
            group(GROUPS - 1, last=True)
            g = GROUPS - 1
            sT_step(g, SLOTS_PER_GROUP - 1)
            h_step(g, 7)
            norm_stats(g)
            norm_rstd(g)
            norm_out(g)

            def general(b):
                for l in range(LAYERS):
                    dve.wait_ge(g_uv, 2 * b + l + 1)
                    V.tensor_tensor(uvg[:, 0:D], PU[:, 0:D], b1row[:, l, :], ALU.add)
                    V.tensor_copy(uvg[:, D:2 * D], PU[:, D:2 * D]).then_inc(g_uv_ok, 1)
                    with dve.Fori(0, STEPS) as i:
                        dve.wait_ge(g_uv_ok, 2 * b + l + 1)
                        n = (b * LAYERS + l) * STEPS + i + 1
                        u = uvg[:, 0:D].rearrange("p (r d) -> p r d", r=1).broadcast_to((128, 4, D))
                        pickrow = ident[:, bass.ds(4 * i, 4)].rearrange("p (r d) -> p r d", d=1).broadcast_to((128, 4, D))
                        V.tensor_tensor(spread[:, :, :], u, pickrow, ALU.mult).then_inc(g_spread_ok, 1)
                        dve.wait_ge(g_rows, n)
                        v = uvg[:, D:2 * D].rearrange("p (r d) -> p r d", r=1).broadcast_to((128, 4, D))
                        V.tensor_tensor(pairs[:, :, :], Z[0][:, :, :], v, ALU.add).then_inc(g_pairs_ok, 1)
                    h = (xT, hT)[l]
                    V.scalar_tensor_tensor(out=baseg[:, :], in0=rowsum[:, 0, :], scalar=b2col[:, l:l + 1],
                                           in1=h[:, 0, :], op0=ALU.mult, op1=ALU.add).then_inc(g_base_ok, 1)
                    dve.wait_ge(g_base_ok, 3 * b + l + 1)
                    if l == 1:
                        V.tensor_tensor(baseg[:, :], baseg[:, :], xT[:, 0, :], ALU.add).then_inc(g_base_ok, 1)
                        dve.wait_ge(g_base_ok, 3 * b + 3)
                    dve.wait_ge(g_msg, 2 * b + l + 1)
                    V.tensor_tensor(hT[:, 0, :], PM[:, 0:128], baseg[:, :], ALU.add).then_inc(g_h_ok, 1)
                dve.wait_ge(g_y_ok, b + 1)
                V.bn_stats(stats[:, 0, :], y[:, 0, :]).then_inc(g_stats_ok, 1)
                dve.wait_ge(g_stats_ok, b + 1)
                V.memset(varE[:, :], 0.0)
                V.bn_aggr(meanvar[:, 0, :], stats[:, 0, :]).then_inc(g_mv_ok, 1)
                dve.wait_ge(g_mv_ok, b + 1)
                V.tensor_scalar(varE[:, 0:1], meanvar[:, 0, 1:2], EPS, None, ALU.add).then_inc(g_var_ok, 1)
                dve.wait_ge(g_root_ok, b + 1)
                rstd_step(1, GROUPS + b)
                dve.wait_ge(g_stored, 16 * (b + 1))
                V.tensor_scalar(outs[:, 0, :], y[:, 0, :], meanvar[:, 0, 0:1], rstd[:, 0:1],
                                ALU.subtract, ALU.mult).then_inc(g_out_ok, 1)

            with dve.If(overflow(dve) > 0):
                dve.wait_ge(outs_free, 16 * (GROUPS + 1))
                V.memset(onesf[:, :], 1.0).then_inc(onesf_ok, 1)
                V.memset(outs[:, 0, :], 0.0).then_inc(g_stored, 16)
                with dve.Fori(0, GRAPHS) as b:
                    general(b)


_INS = ['x', 'adj', 'L0_gnn_w1', 'L0_gnn_b1', 'L0_gnn_w2', 'L0_gnn_b2']


def kernel(**inputs):
    import numpy as _np
    import concourse.bacc as _bacc
    from concourse import mybir as _mybir
    from concourse.bass_utils import run_bass_kernel_spmd as _run

    nc = _bacc.Bacc("TRN2", target_bir_lowering=False, num_devices=1)
    cf, cb = constants()
    arrays, args = {}, []
    for name, a in [(n, inputs[n]) for n in _INS] + [('tables_f32', cf), ('tables_bf16', cb)]:
        a = _np.ascontiguousarray(a)
        arrays[f"in_{name}_dram"] = a
        args.append(nc.dram_tensor(f"in_{name}_dram", a.shape, _mybir.dt.from_np(a.dtype), kind="ExternalInput").ap())
    out = nc.dram_tensor("out_0_dram", (GRAPHS, NODES, D), _mybir.dt.float32, kind="ExternalOutput").ap()
    gnn_kernel(nc, *args, out)
    r = _run(nc, [arrays], core_ids=[0])
    return r.results[0]["out_0_dram"]
```

```python
import numpy as np
import concourse.bass as bass
from concourse import mybir
from contextlib import ExitStack


NODES = 128
D = 128
GRAPHS = 64
LAYERS = 2
GROUP = 4
GROUPS = GRAPHS // GROUP
EPS = 1e-5

REGIONS = [(2, 26), (6, 18), (8, 15), (8, 14), (8, 13), (16, 12), (16, 11), (16, 10), (16, 9), (16, 8), (16, 7)]
SLOTS = sum(r * c for r, c in REGIONS)
TILES = SLOTS // 128
QUADS = -(-TILES // 4)
SLOTS_PER_GROUP = 2 * GROUP
UNITS = SLOTS_PER_GROUP * QUADS
assert sum(r for r, _ in REGIONS) == NODES and SLOTS % 128 == 0


def slot_rows():
    rows, ranks, r0 = [], [], 0
    for n, cap in REGIONS:
        for k in range(cap):
            for i in range(n):
                rows.append(r0 + i)
                ranks.append(k)
        r0 += n
    return np.array(rows), np.array(ranks)


ROWS, RANKS = slot_rows()
WINDOWS = [(int(ROWS[128 * t:128 * t + 128].min()), int(ROWS[128 * t:128 * t + 128].max()) + 1) for t in range(TILES)]
WOFF = [sum(hi - lo for lo, hi in WINDOWS[:t]) for t in range(TILES + 1)]
SPLIT_QUADS = 2
SPLIT = 4 * SPLIT_QUADS
SPLIT_ROWS = max(hi for _, hi in WINDOWS[:SPLIT])
SPLIT_W = 3 * WOFF[SPLIT]
WHOLE_W = WOFF[-1] - WOFF[SPLIT]
assert QUADS == 3 and SPLIT_W <= 512
BLOCKS = [*range(0, NODES, 32), *range(16, NODES - 16, 32)]
EVEN = NODES // 32
BLOCK_OF = [next(n for n, r in enumerate(BLOCKS) if r <= lo and hi <= r + 32) for lo, hi in WINDOWS]


def constants():
    def bits(a):
        return (np.ascontiguousarray(a, np.float32).view(np.uint32) >> 16).astype(np.uint16)
    p = np.arange(128)
    caps = np.zeros(128)
    np.maximum.at(caps, ROWS, RANKS + 1)
    mask = np.zeros((128, SPLIT_W + WHOLE_W))
    for t, (lo, hi) in enumerate(WINDOWS):
        row = ROWS[128 * t:128 * t + 128] - lo
        if t < SPLIT:
            for part in range(3):
                mask[p, 3 * WOFF[t] + part * (hi - lo) + row] = 1
        else:
            mask[p, SPLIT_W + WOFF[t] - WOFF[SPLIT] + row] = 1
    pick = np.zeros((128, TILES, 128))
    pick[96:99] = 1
    for t in range(TILES):
        for e in range(128):
            r = ROWS[128 * t + e] - BLOCKS[BLOCK_OF[t]]
            pick[3 * r:3 * r + 3, t, e] = 1
    tie = (127 - p) / 128
    f = [np.eye(128), np.broadcast_to(p, (128, 128)), np.broadcast_to(caps, (128, 128)), tie[:, None], mask]
    b = [np.eye(128), np.triu(np.ones((128, 128))), np.ones((128, 128)), np.tile(np.diag(tie), (1, GROUP)),
         np.broadcast_to(RANKS + 1, (128, SLOTS)), pick.reshape(128, -1)]
    return (np.concatenate([np.asarray(a, np.float32) for a in f], 1),
            np.concatenate([bits(a) for a in b], 1))


def gnn_kernel(nc, x, adj, w1, b1, w2, b2, cf, cb, out):
    f32, bf16, u16 = mybir.dt.float32, mybir.dt.bfloat16, mybir.dt.uint16
    ALU, ACT, AX = mybir.AluOpType, mybir.ActivationFunctionType, mybir.AxisListType
    ctx = ExitStack()
    with ctx:
        def sb(name, shape, dt=f32):
            return ctx.enter_context(nc.sbuf_tensor(name, shape, dt))

        def sem(name):
            return ctx.enter_context(nc.semaphore(name))

        CF = sb("CF", [128, cf.shape[1]])
        CB = sb("CB", [128, cb.shape[1]], bf16)
        ident, iota, caps, tie = CF[:, 0:128], CF[:, 128:256], CF[:, 256:384], CF[:, 384:385]
        mask = CF[:, 385:385 + SPLIT_W + WHOLE_W]
        SMALL_F, SMALL_B = 385, 896
        identb, upto, onesb, tiediag = CB[:, 0:128], CB[:, 128:256], CB[:, 256:384], CB[:, 384:384 + 512]
        rankc = CB[:, 896:896 + SLOTS]
        pick = CB[:, 896 + SLOTS:].rearrange("p (n e) -> p n e", e=128)
        w1_in = sb("w1_in", [128, LAYERS, 2 * D])
        w2_in = sb("w2_in", [128, LAYERS, D])
        w1T = sb("w1T", [128, LAYERS, 2 * D])
        w2T = sb("w2T", [128, LAYERS, D])
        b1row = sb("b1row", [128, LAYERS, D])
        b2col = sb("b2col", [128, LAYERS])

        adj_in = sb("adj_in", [128, GROUP, NODES])
        x_in = sb("x_in", [128, GROUP, D])
        junk = sb("junk", [128, GROUP, 128], bf16)
        deg = sb("deg", [128, GROUP])
        key = sb("key", [128, GROUP])
        degdiag = sb("degdiag", [128, GROUP, 128], bf16)
        above = sb("above", [128, GROUP, 128], bf16)
        place = sb("place", [128, GROUP])
        perm = sb("perm", [128, GROUP, 128])
        permT = sb("permT", [128, GROUP, 128])
        adj1 = sb("adj1", [128, GROUP, 128])
        adj2 = sb("adj2", [128, GROUP, 128])
        adjrest = sb("adjrest", [128, GROUP, 128])
        adjp = sb("adjp", [128, 3, GROUP, 128], bf16)
        nz = sb("nz", [128, GROUP, 128], bf16)
        rank = sb("rank", [128, GROUP, 128], bf16)
        over = sb("over", [128, GROUPS])
        xT = sb("xT", [128, GROUP, 128])
        rowsum = sb("rowsum", [128, GROUP, 128])
        base0 = sb("base0", [128, GROUP, 128])
        base1 = sb("base1", [128, GROUP, 128])
        take = sb("take", [128, GROUP, SLOTS], bf16)
        Wparts = sb("Wparts", [128, GROUP, SPLIT_W], bf16)
        W = sb("W", [128, GROUP, WHOLE_W])
        uvrest = [sb(f"uvrest{i}", [128, 2 * D]) for i in range(2)]
        parts = sb("parts", [128, SLOTS_PER_GROUP, 3, 2 * D], bf16)
        ustack = sb("ustack", [128, SLOTS_PER_GROUP, len(BLOCKS), D], bf16)
        b1parts = sb("b1parts", [128, 3, LAYERS, D], bf16)
        b1rest = sb("b1rest", [128, LAYERS, D])
        b1mix = [sb(f"b1mix{i}", [128, LAYERS, D], bf16) for i in range(3)]
        m = sb("m", [128, 4, D])
        mparts = [[sb(f"mparts{k}{i}", [128, 3, 4, D], bf16) for i in range(2)] for k in range(SPLIT_QUADS)]
        mrest = [sb(f"mrest{k}", [128, 4, D]) for k in range(SPLIT_QUADS)]
        sT = [sb(f"sT{i}", [128, 128]) for i in range(2)]
        hT = sb("hT", [128, GROUP, 128])
        hsum = sb("hsum", [128, GROUP, 128])
        yT = [sb(f"yT{i}", [128, 128]) for i in range(2)]
        yp = [sb(f"yp{i}", [128, 128]) for i in range(2)]
        y = sb("y", [128, GROUP, D])
        stats = sb("stats", [128, GROUP, 6])
        meanvar = sb("meanvar", [128, GROUP, 2])
        varE = sb("varE", [128, GROUP])
        rstd = sb("rstd", [128, GROUP])
        root, inv, quot, twice, half = [sb(n, [128, GROUP]) for n in "root inv quot twice half".split()]
        outs = sb("outs", [128, GROUP, D])

        Z = [ctx.enter_context(nc.psum_tensor(f"Z{i}", [128, 4, D], f32)) for i in range(3)]
        PS = ctx.enter_context(nc.psum_tensor("PS", [128, 4, 128], f32))
        PU = ctx.enter_context(nc.psum_tensor("PU", [128, 512], f32))
        PM = ctx.enter_context(nc.psum_tensor("PM", [128, 512], f32))
        PA = ctx.enter_context(nc.psum_tensor("PA", [128, GROUP, 128], f32))
        PB = ctx.enter_context(nc.psum_tensor("PB", [128, GROUP, 128], f32))

        const_in, tables_in, w_in, adj_loaded, x_loaded, outs_free = map(
            sem, "const_in tables_in w_in adj_loaded x_loaded outs_free".split())
        stacked = [sem(f"stacked{s}") for s in range(SLOTS_PER_GROUP)]
        spilled = [sem(f"spilled{s}") for s in range(SLOTS_PER_GROUP)]
        bounce = [nc.dram_tensor(f"bounce{s}", (NODES * 3, D), bf16, kind="Internal").ap()
                  for s in range(SLOTS_PER_GROUP)]
        (wT_done, key_done, permT_done, adj1_done, adj2_done, rank_done, rowsum_done, xT_done, value_done, uv_done,
         z_done, sum_done, msg_done, yp_done, y_done) = [sem(f"pe_{s}") for s in (
            "wT key permT adj1 adj2 rank rowsum xT value uv z sum msg yp y".split())]
        (deg_ok, key_ok, above_ok, place_ok, perm_ok, nz_ok, adjrest_ok, adjlo_ok, rank_ok, over_ok, base_ok,
         take_ok, W_ok, sT_ok, uvrest_ok, hT_ok, stats_ok, mv_ok, varE_ok, outs_ok,
         inv_ok, quot_ok, twice_ok, half_ok, rstd_ok) = [sem(f"dve_{s}") for s in (
            "deg key above place perm nz adjrest adjlo rank over base take W sT uvrest hT "
            "stats mv varE outs inv quot twice half rstd".split())]
        uvlo_ok, hsum_ok, diag_ok = [sem(f"pool_{s}") for s in "uvlo hsum diag".split()]
        b1_ok = [sem(f"dve_b1_{i}") for i in range(7)]
        mhi_ok, mmid_ok, mrest_ok, mlo_ok = [[sem(f"{s}{k}") for k in range(SPLIT_QUADS)] for s in (
            "act_mhi act_mmid dve_mrest pool_mlo".split())]
        (wT_ok, permT_ok, adj1_ok, adj2_ok, adjhi_ok, adjmid_ok, rowsum_ok, xT_ok, uvhi_ok, uvmid_ok, m_ok,
         yp_ok, y_ok, root_ok, table_ok) = [sem(f"act_{s}") for s in (
            "wT permT adj1 adj2 adjhi adjmid rowsum xT uvhi uvmid m yp y root table".split())]

        spread = sb("spread", [128, 4, D])
        pairs = sb("pairs", [128, 4, D])
        messages = sb("messages", [128, 4, D])
        uvg = sb("uvg", [128, 2 * D])
        baseg = sb("baseg", [128, 128])
        onesf = sb("onesf", [128, 128])
        overs = sb("overs", [128, 1])
        some = sb("some", [128, 1], bf16)
        flag = sb("flag", [128, 1], mybir.dt.int32)
        (overs_ok, some_ok, count_done, flag_ok) = [sem(s) for s in "dve_overs dve_some pe_count dve_flag".split()]
        (g_loaded, g_turned, g_turned_ok, g_uv, g_uv_ok, g_spread_ok, g_rows, g_pairs_ok, g_messages_ok, g_sum, g_sT_ok,
         g_base_ok, g_msg, g_h_ok, g_back, g_y_ok, g_stats_ok, g_mv_ok, g_var_ok, g_root_ok, g_out_ok, g_stored,
         onesf_ok) = [sem(f"general_{s}") for s in (
            "loaded turned turned_ok uv uv_ok spread_ok rows pairs_ok messages_ok sum sT_ok base_ok msg h_ok back y_ok "
            "stats_ok mv_ok var_ok root_ok out_ok stored ones".split())]
        STEPS = NODES // 4

        def overflow(eng):
            eng.wait_ge(flag_ok, 1)
            return eng.value_load(flag[0:1, 0:1], min_val=0, max_val=128)

        x_v = x.rearrange("b n d -> n b d")
        adj_v = adj.rearrange("b n j -> n b j")
        out_v = out.rearrange("b n d -> n b d")
        block = ctx.enter_context(nc.Block())

        @block.sync
        def _(sp):
            def start_of(g):
                return g * GROUP if isinstance(g, int) else sp.snap(g * GROUP)

            def load(g, at):
                sp.wait_ge(adj1_done, g)
                sp.wait_ge(xT_done, g)
                sp.dma_start(adj_in[:, :, :], adj_v[:, bass.ds(at, GROUP), :]).then_inc(adj_loaded, 16)
                sp.dma_start(x_in[:, :, :], x_v[:, bass.ds(at, GROUP), :]).then_inc(x_loaded, 16)

            def stack(g, s):
                k = g * SLOTS_PER_GROUP + s
                sp.wait_ge(uvlo_ok, k + 1)
                sp.wait_ge(uvhi_ok, k + 1)
                sp.wait_ge(uvmid_ok, k + 1)
                sp.dma_start(bounce[s].rearrange("(i p) d -> i p d", p=3), parts[:, s, :, 0:D]).then_inc(spilled[s], 16)
                sp.wait_ge(spilled[s], 16 * (g + 1))
                odd = bounce[s][3 * 16:3 * (NODES - 16), :]
                sp.dma_start(ustack[0:96, s, 0:EVEN, :], bounce[s].rearrange("(b k) d -> k b d", k=96)).then_inc(stacked[s], 16)
                sp.dma_start(ustack[0:96, s, EVEN:, :], odd.rearrange("(b k) d -> k b d", k=96)).then_inc(stacked[s], 16)

            def store(g, at):
                sp.wait_ge(outs_ok, g + 1)
                sp.dma_start(out_v[:, bass.ds(at, GROUP), :], outs[:, :, :]).then_inc(outs_free, 16)

            def group(g, first=False, last=False, load_next=True):
                before = 0 if first else start_of(g - 1)
                after = start_of(g + 2)
                for q in range(GROUP):
                    stack(g, GROUP + q)
                    if q == 1 and not first:
                        store(g - 1, before)
                if load_next:
                    load(g + 2, after)
                if not last:
                    for q in range(GROUP):
                        stack(g + 1, q)

            sp.dma_start(adj_in[:, :, :], adj_v[:, 0:GROUP, :]).then_inc(adj_loaded, 16)
            sp.dma_start(CF[:, 0:SMALL_F], cf[:, 0:SMALL_F]).then_inc(const_in, 16)
            sp.dma_start(CB[:, 0:SMALL_B].bitcast(u16), cb[:, 0:SMALL_B]).then_inc(const_in, 16)
            sp.dma_start(x_in[:, :, :], x_v[:, 0:GROUP, :]).then_inc(x_loaded, 16)
            sp.dma_start(w1_in[:, :, :], w1.rearrange("l o c -> o l c")).then_inc(w_in, 16)
            sp.dma_start(w2_in[:, :, :], w2.rearrange("l o c -> o l c")).then_inc(w_in, 16)
            sp.dma_start(b1row[:, :, :], b1.rearrange("(a l) d -> a l d", a=1).broadcast_to((128, LAYERS, D)))\
              .then_inc(w_in, 16)
            sp.dma_start(b2col[:, :], b2.rearrange("l d -> d l"), allow_slow_non_contiguous=True).then_inc(w_in, 16)
            sp.dma_start(CB[:, SMALL_B:].bitcast(u16), cb[:, SMALL_B:]).then_inc(tables_in, 16)
            sp.dma_start(CF[:, SMALL_F:], cf[:, SMALL_F:]).then_inc(tables_in, 16)
            load(1, GROUP)
            for q in range(GROUP):
                stack(0, q)
            group(0, first=True)
            with sp.Fori(1, GROUPS - 2) as g:
                group(g)
            group(GROUPS - 2, load_next=False)
            group(GROUPS - 1, last=True, load_next=False)
            store(GROUPS - 1, GRAPHS - GROUP)
            sp.wait_ge(outs_free, 16 * (GROUPS + 1))

            def general(b):
                at = sp.snap(b)
                sp.dma_start(adj_in[:, 0, :], adj_v[:, bass.ds(at, 1), :].rearrange("n b j -> n (b j)")).then_inc(g_loaded, 16)
                sp.dma_start(x_in[:, 0, :], x_v[:, bass.ds(at, 1), :].rearrange("n b d -> n (b d)")).then_inc(g_loaded, 16)
                sp.wait_ge(g_out_ok, b + 1)
                sp.dma_start(out_v[:, bass.ds(at, 1), :].rearrange("n b d -> n (b d)"), outs[:, 0, :]).then_inc(g_stored, 16)

            with sp.If(overflow(sp) > 0):
                with sp.Fori(0, GRAPHS) as b:
                    general(b)
                sp.wait_ge(g_stored, 16 * (GRAPHS + 1))

        @block.tensor
        def _(pe):
            mm = nc.tensor.matmul

            def sum_whole(g, s, t):
                q = s % GROUP
                if t == SPLIT:
                    pe.wait_ge(W_ok, g * GROUP + q + 1)
                    pe.wait_ge(sT_ok, g * SLOTS_PER_GROUP + s)
                    pe.wait_ge(m_ok, g * SLOTS_PER_GROUP + s + 1)
                lo, hi = WINDOWS[t]
                product = mm(PS[:, 0, lo:hi], m[:, t % 4, :], W[:, q, WOFF[t] - WOFF[SPLIT]:WOFF[t + 1] - WOFF[SPLIT]],
                             start=(t == SPLIT), stop=False, skip_group_check=True)
                if t == TILES - 1:
                    product.then_inc(sum_done, 1)

            def z_unit(g, n, before=None):
                s, k = divmod(n, QUADS)
                q = s % GROUP
                if k == 0:
                    pe.wait_ge(uvlo_ok, g * SLOTS_PER_GROUP + s + 1)
                    pe.wait_ge(uvhi_ok, g * SLOTS_PER_GROUP + s + 1)
                    pe.wait_ge(uvmid_ok, g * SLOTS_PER_GROUP + s + 1)
                    pe.wait_ge(stacked[s], 32 * (g + 1))
                    if s < GROUP:
                        pe.wait_ge(take_ok, g * GROUP + q + 1)
                if s or not isinstance(g, int) or g:
                    pe.wait_ge(mrest_ok[k] if k < SPLIT_QUADS else m_ok, g * SLOTS_PER_GROUP + s)
                for t in range(4 * k, min(4 * k + 4, TILES)):
                    o = Z[k][:, t % 4, :]
                    lhs = take[:, q, 128 * t:128 * t + 128]
                    for p in range(3):
                        mm(o, lhs, parts[:, s, p, D:2 * D], start=(p == 0), stop=False)
                    last = mm(o, pick[0:99, t, :], ustack[0:99, s, BLOCK_OF[t], :], start=False, stop=True)
                    if t == min(4 * k + 4, TILES) - 1:
                        last.then_inc(z_done, 1)
                    elif before is not None and SPLIT + 1 + t % 4 < TILES:
                        sum_whole(*before, SPLIT + 1 + t % 4)

            def sum_parts(g, s, k):
                q = s % GROUP
                pe.wait_ge(mlo_ok[k], g * SLOTS_PER_GROUP + s + 1)
                pe.wait_ge(mhi_ok[k], g * SLOTS_PER_GROUP + s + 1)
                pe.wait_ge(mmid_ok[k], g * SLOTS_PER_GROUP + s + 1)
                for t in range(4 * k, 4 * k + 4):
                    lo, hi = WINDOWS[t]
                    values = Wparts[:, q, 3 * WOFF[t]:3 * WOFF[t + 1]].rearrange("p (v i) -> p v i", v=3)
                    for p in range(3):
                        last = mm(PS[:, 0:3, lo:hi], mparts[k][s % 2][:, p, t % 4, :], values, start=False,
                                  stop=(t == SPLIT - 1 and p == 2), skip_group_check=True)
                last.then_inc(sum_done, 1)

            def msg(g, s):
                pe.wait_ge(sT_ok, g * SLOTS_PER_GROUP + s + 1)
                if 1 <= s <= GROUP:
                    pe.wait_ge(hT_ok, g * SLOTS_PER_GROUP + s)
                else:
                    pe.wait_ge(y_ok, g * GROUP + max(0, s - GROUP))
                mm(PM[:, 0:128], w2T[:, s // GROUP, :], sT[s % 2][:, :], start=True, stop=True).then_inc(msg_done, 1)

            def yp_step(g, q):
                pe.wait_ge(hT_ok, g * SLOTS_PER_GROUP + GROUP + q + 1)
                nc.tensor.transpose(PM[:, 0:128], yT[q % 2][:, :], ident).then_inc(yp_done, 1)

            def y_step(g, q):
                pe.wait_ge(yp_ok, g * GROUP + q + 1)
                if q == 0:
                    pe.wait_ge(permT_ok, g + 1)
                mm(PM[:, 0:128], permT[:, q, :], yp[q % 2][:, :], start=True, stop=True).then_inc(y_done, 1)

            def uv_step(g, s):
                k = g * SLOTS_PER_GROUP + s
                pe.wait_ge(uvrest_ok, k)
                if s < GROUP:
                    pe.wait_ge(xT_ok, g + 1)
                    h = xT
                else:
                    pe.wait_ge(hT_ok, k - GROUP + 1)
                    h = hT
                mm(PU[:, 0:2 * D], h[:, s % GROUP, :], w1T[:, s // GROUP, :], start=True, stop=True)\
                    .then_inc(uv_done, 1)

            def key_step(g):
                pe.wait_ge(diag_ok, g + 1)
                pe.wait_ge(W_ok, max(0, (g - 1) * GROUP + 3) if isinstance(g, int) else (g - 1) * GROUP + 3)
                o = PA[:, :, :].rearrange("p q i -> p (q i)")
                mm(o, onesb, degdiag[:, :, :].rearrange("p q i -> p (q i)"), start=True, stop=False)
                mm(o, onesb, tiediag, start=False, stop=True).then_inc(key_done, 1)

            def permT_step(g):
                pe.wait_ge(perm_ok, g + 1)
                pe.wait_ge(W_ok, g * GROUP + 3)
                for q in range(GROUP):
                    last = nc.tensor.transpose(PB[:, q, :], perm[:, q, :], ident)
                last.then_inc(permT_done, 1)

            def adj1_step(g):
                pe.wait_ge(perm_ok, g + 1)
                pe.wait_ge(above_ok, g + 1)
                pe.wait_ge(W_ok, g * GROUP)
                for q in range(GROUP):
                    last = mm(PA[:, q, :], adj_in[:, q, :], perm[:, q, :], start=True, stop=True)
                last.then_inc(adj1_done, 1)

            def adj2_step(g):
                pe.wait_ge(adj1_ok, g + 1)
                for q in range(GROUP):
                    last = mm(PA[:, q, :], perm[:, q, :], adj1[:, q, :], start=True, stop=True)
                last.then_inc(adj2_done, 1)

            def rank_step(g):
                pe.wait_ge(nz_ok, g + 1)
                pe.wait_ge(xT_ok, g + 1)
                mm(PB[:, :, :].rearrange("p q i -> p (q i)"), upto, nz[:, :, :].rearrange("p q i -> p (q i)"),
                   start=True, stop=True).then_inc(rank_done, 1)

            def rowsum_step(g):
                pe.wait_ge(adjlo_ok, g + 1)
                pe.wait_ge(adjhi_ok, g + 1)
                pe.wait_ge(adjmid_ok, g + 1)
                pe.wait_ge(adj2_ok, g + 1)
                for p in range(3):
                    last = mm(PA[:, :, :].rearrange("p q i -> p (q i)"), onesb,
                              adjp[:, p, :, :].rearrange("p q i -> p (q i)"), start=(p == 0), stop=(p == 2))
                last.then_inc(rowsum_done, 1)

            def xT_step(g):
                pe.wait_ge(perm_ok, g + 1)
                pe.wait_ge(x_loaded, 16 * (g + 1))
                pe.wait_ge(W_ok, g * GROUP)
                for q in range(GROUP):
                    last = mm(PB[:, q, :], x_in[:, q, :], perm[:, q, :], start=True, stop=True)
                last.then_inc(xT_done, 1)

            def value_step(g, q, last=False):
                pe.wait_ge(take_ok, g * GROUP + q + 1)
                if q == 0:
                    pe.wait_ge(rowsum_ok, g + 1)
                    pe.wait_ge(over_ok, g + 1)
                elif q < 3:
                    pe.wait_ge(W_ok, g * GROUP + q)
                else:
                    pe.wait_ge(permT_ok, g + 1)
                    if last:
                        pe.wait_ge(W_ok, g * GROUP + q)
                    else:
                        pe.wait_ge(above_ok, g + 2)
                split, whole = [bank[:, :, :].rearrange("p q i -> p (q i)") for bank in (PA, PB)]
                for t, (lo, hi) in enumerate(WINDOWS):
                    lhs = take[:, q, 128 * t:128 * t + 128]
                    if t < SPLIT:
                        o = split[:, 3 * WOFF[t]:3 * WOFF[t + 1]].rearrange("p (v i) -> p v i", v=3)
                        mm(o, lhs, adjp[:, 0:3, q, lo:hi], start=True, stop=True)
                    else:
                        for p in range(3):
                            final = mm(whole[:, WOFF[t] - WOFF[SPLIT]:WOFF[t + 1] - WOFF[SPLIT]], lhs, adjp[:, p, q, lo:hi],
                                       start=(p == 0), stop=(p == 2))
                final.then_inc(value_done, 1)

            def group(g, first=False, last=False):
                for n in range(UNITS):
                    slot = (g, n // QUADS - 1) if n >= QUADS else None if first else (g - 1, 7)
                    z_unit(g, n, slot if n % QUADS == 1 else None)
                    if n % QUADS == 0 and n < 6 * QUADS: uv_step(g, n // QUADS + 2)
                    if n % QUADS == 0 and n >= 6 * QUADS and not last: uv_step(g + 1, n // QUADS - 6)
                    if n in (0, 3) and not first: yp_step(g - 1, 2 + n // QUADS)
                    if n in (18, 21): yp_step(g, n // QUADS - 6)
                    if n % QUADS == 0 and slot: sum_whole(*slot, SPLIT)
                    if n % QUADS < SPLIT_QUADS and slot: sum_parts(*slot, n % QUADS)
                    if n == 1 and not first: y_step(g - 1, 2)
                    if n == 0 and first: value_step(g, 1)
                    if n == 1: value_step(g, 2)
                    if n == 2 and not first: msg(g - 1, 7)
                    if n == 4 and not first: y_step(g - 1, 3)
                    if n == 4 and not last: key_step(g + 1)
                    if n == 4: permT_step(g)
                    if n == 5: msg(g, 0)
                    if n == 6: value_step(g, 3, last)
                    if n == 8: msg(g, 1)
                    if n == 8 and not last: adj1_step(g + 1)
                    if n == 8 and not last: xT_step(g + 1)
                    if n == 10 and not last: adj2_step(g + 1)
                    if n == 11: msg(g, 2)
                    if n == 13 and not last: rank_step(g + 1)
                    if n == 14: msg(g, 3)
                    if n == 16 and not last: rowsum_step(g + 1)
                    if n == 17: msg(g, 4)
                    if n == 19: y_step(g, 0)
                    if n == 19 and not last: value_step(g + 1, 0)
                    if n == 20: msg(g, 5)
                    if n == 22: y_step(g, 1)
                    if n == 22 and not last: value_step(g + 1, 1)
                    if n == 23: msg(g, 6)
                    if n == 8 and last:
                        pe.wait_ge(some_ok, 1)
                        pe.wait_ge(W_ok, (g + 1) * GROUP)
                        mm(PA[:, 0, 0:1], onesb, some[:, :], start=True, stop=True).then_inc(count_done, 1)

            pe.wait_ge(const_in, 32)
            key_step(0)
            pe.wait_ge(w_in, 64)
            for l in range(LAYERS):
                nc.tensor.transpose(PB[:, 2 * l, :], w1_in[:, l, 0:D], ident)
                nc.tensor.transpose(PB[:, 2 * l + 1, :], w1_in[:, l, D:2 * D], ident)
            for l in range(LAYERS):
                last = nc.tensor.transpose(PM[:, 128 * l:128 * l + 128], w2_in[:, l, :], ident)
            last.then_inc(wT_done, 1)
            adj1_step(0)
            pe.wait_ge(wT_ok, 2)
            xT_step(0)
            adj2_step(0)
            uv_step(0, 0)
            rank_step(0)
            uv_step(0, 1)
            rowsum_step(0)
            value_step(0, 0)
            pe.wait_ge(b1_ok[6], 1 + LAYERS)
            group(0, first=True)
            with pe.Fori(1, GROUPS - 1) as g:
                group(g)
            group(GROUPS - 1, last=True)
            g = GROUPS - 1
            sum_whole(g, 7, SPLIT)
            sum_parts(g, 7, 0)
            for t in range(SPLIT + 1, TILES):
                sum_whole(g, 7, t)
            yp_step(g, 2)
            sum_parts(g, 7, 1)
            y_step(g, 2)
            msg(g, 7)
            yp_step(g, 3)
            y_step(g, 3)

            def general(b):
                pe.wait_ge(g_loaded, 32 * (b + 1))
                nc.tensor.transpose(PA[:, 0, :], adj_in[:, 0, :], ident)
                nc.tensor.transpose(PA[:, 1, :], x_in[:, 0, :], ident).then_inc(g_turned, 1)
                pe.wait_ge(g_turned_ok, 2 * b + 1)
                mm(PA[:, 2, :], onesf[:, :], adj1[:, 0, :], start=True, stop=True).then_inc(g_turned, 1)
                for l in range(LAYERS):
                    h = (xT, hT)[l]
                    if l == 0:
                        pe.wait_ge(g_turned_ok, 2 * b + 2)
                    else:
                        pe.wait_ge(g_h_ok, 2 * b + 1)
                    mm(PU[:, 0:2 * D], h[:, 0, :], w1T[:, l, :], start=True, stop=True).then_inc(g_uv, 1)
                    with pe.Fori(0, STEPS) as i:
                        n = (b * LAYERS + l) * STEPS + i + 1
                        pe.wait_ge(g_spread_ok, n)
                        mm(Z[0][:, :, :].rearrange("p r d -> p (r d)"), onesf[:, :],
                           spread[:, :, :].rearrange("p r d -> p (r d)"), start=True, stop=True).then_inc(g_rows, 1)
                        pe.wait_ge(g_messages_ok, n)
                        for r in range(4):
                            last = mm(PS[:, 0, bass.ds(4 * i + r, 1)], messages[:, r, :], adj1[:, 0, bass.ds(4 * i + r, 1)],
                                      start=True, stop=True)
                        last.then_inc(g_sum, 1)
                    pe.wait_ge(g_sT_ok, 2 * b + l + 1)
                    mm(PM[:, 0:128], w2T[:, l, :], sT[0][:, :], start=True, stop=True).then_inc(g_msg, 1)
                pe.wait_ge(g_h_ok, 2 * b + 2)
                nc.tensor.transpose(PM[:, 0:128], hT[:, 0, :], ident).then_inc(g_back, 1)

            with pe.If(overflow(pe) > 0):
                pe.wait_ge(onesf_ok, 1)
                with pe.Fori(0, GRAPHS) as b:
                    general(b)

        @block.scalar
        def _(act):
            def copy(o, i):
                return nc.scalar.activation(o, i, ACT.Copy)

            def relu_unit(g, n):
                s, k = divmod(n, QUADS)
                slot = g * SLOTS_PER_GROUP + s
                act.wait_ge(z_done, g * UNITS + n + 1)
                if k < SPLIT_QUADS:
                    if s >= 2 or not isinstance(g, int) or g:
                        act.wait_ge(sum_done, QUADS * (slot - 1))
                    nc.scalar.activation(mparts[k][s % 2][:, 0, :, :], Z[k][:, :, :], ACT.Relu).then_inc(mhi_ok[k], 1)
                else:
                    if s or not isinstance(g, int) or g:
                        act.wait_ge(sum_done, QUADS * (slot - 1) + 2)
                    tiles = TILES - 4 * k
                    nc.scalar.activation(m[:, 0:tiles, :], Z[k][:, 0:tiles, :], ACT.Relu).then_inc(m_ok, 1)

            def mmid_step(g, s, k):
                act.wait_ge(mrest_ok[k], g * SLOTS_PER_GROUP + s + 1)
                copy(mparts[k][s % 2][:, 1, :, :], mrest[k][:, :, :]).then_inc(mmid_ok[k], 1)

            def yp_copy(g, q):
                act.wait_ge(yp_done, g * GROUP + q + 1)
                if q >= 2 or not isinstance(g, int) or g:
                    act.wait_ge(y_done, g * GROUP + q - 1)
                copy(yp[q % 2][:, :], PM[:, 0:128]).then_inc(yp_ok, 1)

            def y_copy(g, q):
                act.wait_ge(y_done, g * GROUP + q + 1)
                if q == 0:
                    act.wait_ge(outs_ok, g)
                copy(y[:, q, :], PM[:, 0:128]).then_inc(y_ok, 1)

            def hi_step(g, s):
                k = g * SLOTS_PER_GROUP + s
                act.wait_ge(uv_done, k + 1)
                if not isinstance(g, int) or g:
                    act.wait_ge(z_done, (g - 1) * UNITS + (s + 1) * QUADS)
                    act.wait_ge(stacked[s], 32 * g)
                copy(parts[:, s, 0, :], PU[:, 0:2 * D]).then_inc(uvhi_ok, 1)

            def mid_step(g, s):
                act.wait_ge(uvrest_ok, g * SLOTS_PER_GROUP + s + 1)
                copy(parts[:, s, 1, :], uvrest[s % 2][:, :]).then_inc(uvmid_ok, 1)

            def permT_copy(g):
                act.wait_ge(permT_done, g + 1)
                act.wait_ge(y_done, g * GROUP)
                copy(permT[:, :, :], PB[:, :, :]).then_inc(permT_ok, 1)

            def adj1_copy(g):
                act.wait_ge(adj1_done, g + 1)
                act.wait_ge(adj2_done, g)
                copy(adj1[:, :, :], PA[:, :, :]).then_inc(adj1_ok, 1)

            def adj2_copy(g):
                act.wait_ge(adj2_done, g + 1)
                act.wait_ge(nz_ok, g)
                act.wait_ge(adjrest_ok, g)
                copy(adj2[:, :, :], PA[:, :, :]).then_inc(adj2_ok, 1)

            def adjhi_step(g):
                act.wait_ge(adj2_ok, g + 1)
                act.wait_ge(value_done, g * GROUP)
                act.wait_ge(rowsum_done, g)
                copy(adjp[:, 0, :, :], adj2[:, :, :]).then_inc(adjhi_ok, 1)

            def adjmid_step(g):
                act.wait_ge(adjrest_ok, g + 1)
                copy(adjp[:, 1, :, :], adjrest[:, :, :]).then_inc(adjmid_ok, 1)

            def rowsum_copy(g):
                act.wait_ge(rowsum_done, g + 1)
                act.wait_ge(base_ok, 2 * g)
                copy(rowsum[:, :, :], PA[:, :, :]).then_inc(rowsum_ok, 1)

            def xT_copy(g):
                act.wait_ge(xT_done, g + 1)
                act.wait_ge(base_ok, 2 * g)
                if not isinstance(g, int) or g:
                    act.wait_ge(uv_done, (g - 1) * SLOTS_PER_GROUP + GROUP)
                copy(xT[:, :, :], PB[:, :, :]).then_inc(xT_ok, 1)

            def root_step(g):
                act.wait_ge(varE_ok, g + 1)
                nc.scalar.activation(root[:, :], varE[:, :], ACT.Sqrt).then_inc(root_ok, 1)

            def group(g, first=False, last=False):
                for n in range(UNITS):
                    relu_unit(g, n)
                    if n % QUADS == 0 and n < 6 * QUADS: hi_step(g, n // QUADS + 2)
                    if n % QUADS == 0 and n >= 6 * QUADS and not last: hi_step(g + 1, n // QUADS - 6)
                    if n == 0 and not first: yp_copy(g - 1, 2)
                    if n == 0: mid_step(g, 2)
                    if n == 1: mmid_step(g, 0, 0)
                    if n == 1 and not first: y_copy(g - 1, 2)
                    if n == 2: mmid_step(g, 0, 1)
                    if n == 3 and not first: yp_copy(g - 1, 3)
                    if n == 3: mid_step(g, 3)
                    if n == 4: mmid_step(g, 1, 0)
                    if n == 4 and not first: y_copy(g - 1, 3)
                    if n == 5: mmid_step(g, 1, 1)
                    if n == 5: permT_copy(g)
                    if n == 6: mid_step(g, 4)
                    if n == 7: mmid_step(g, 2, 0)
                    if n == 8: mmid_step(g, 2, 1)
                    if n == 9 and not last: adj1_copy(g + 1)
                    if n == 9 and not last: xT_copy(g + 1)
                    if n == 9: mid_step(g, 5)
                    if n == 10: mmid_step(g, 3, 0)
                    if n == 10 and not first: root_step(g - 1)
                    if n == 11: mmid_step(g, 3, 1)
                    if n == 12 and not last: adj2_copy(g + 1)
                    if n == 12 and not last: adjhi_step(g + 1)
                    if n == 12: mid_step(g, 6)
                    if n == 13: mmid_step(g, 4, 0)
                    if n == 14: mmid_step(g, 4, 1)
                    if n == 14 and not last: adjmid_step(g + 1)
                    if n == 15: mid_step(g, 7)
                    if n == 16: mmid_step(g, 5, 0)
                    if n == 17 and not last: rowsum_copy(g + 1)
                    if n == 17: mmid_step(g, 5, 1)
                    if n == 18: yp_copy(g, 0)
                    if n == 18 and not last: mid_step(g + 1, 0)
                    if n == 19: mmid_step(g, 6, 0)
                    if n == 19: y_copy(g, 0)
                    if n == 20: mmid_step(g, 6, 1)
                    if n == 21: yp_copy(g, 1)
                    if n == 21 and not last: mid_step(g + 1, 1)
                    if n == 22: mmid_step(g, 7, 0)
                    if n == 22: y_copy(g, 1)
                    if n == 23: mmid_step(g, 7, 1)

            act.wait_ge(const_in, 32)
            nc.scalar.activation(root[:, 0:1], iota[:, 0:1], ACT.Sqrt).then_inc(table_ok, 1)
            act.wait_ge(table_ok, 1)
            act.wait_ge(wT_done, 1)
            copy(w1T[:, :, :].rearrange("p l o -> p (l o)"), PB[:, :, :].rearrange("p q i -> p (q i)"))\
                .then_inc(wT_ok, 1)
            copy(w2T[:, :, :].rearrange("p l o -> p (l o)"), PM[:, 0:256]).then_inc(wT_ok, 1)
            adj1_copy(0)
            xT_copy(0)
            adj2_copy(0)
            adjhi_step(0)
            hi_step(0, 0)
            adjmid_step(0)
            mid_step(0, 0)
            hi_step(0, 1)
            mid_step(0, 1)
            rowsum_copy(0)
            group(0, first=True)
            with act.Fori(1, GROUPS - 1) as g:
                group(g)
            group(GROUPS - 1, last=True)
            g = GROUPS - 1
            yp_copy(g, 2)
            y_copy(g, 2)
            yp_copy(g, 3)
            y_copy(g, 3)
            root_step(g)

            def general(b):
                act.wait_ge(g_turned, 2 * b + 1)
                copy(adj1[:, 0, :], PA[:, 0, :]).then_inc(g_turned_ok, 1)
                act.wait_ge(g_turned, 2 * b + 2)
                copy(xT[:, 0, :], PA[:, 1, :])
                copy(rowsum[:, 0, :], PA[:, 2, :]).then_inc(g_turned_ok, 1)
                for l in range(LAYERS):
                    with act.Fori(0, STEPS) as i:
                        act.wait_ge(g_pairs_ok, (b * LAYERS + l) * STEPS + i + 1)
                        nc.scalar.activation(messages[:, :, :], pairs[:, :, :], ACT.Relu).then_inc(g_messages_ok, 1)
                    act.wait_ge(g_sum, (b * LAYERS + l + 1) * STEPS)
                    copy(sT[0][:, :], PS[:, 0, :]).then_inc(g_sT_ok, 1)
                act.wait_ge(g_back, b + 1)
                copy(y[:, 0, :], PM[:, 0:128]).then_inc(g_y_ok, 1)
                act.wait_ge(g_var_ok, b + 1)
                nc.scalar.activation(root[:, 0:1], varE[:, 0:1], ACT.Sqrt).then_inc(g_root_ok, 1)

            with act.If(overflow(act) > 0):
                with act.Fori(0, GRAPHS) as b:
                    general(b)

        @block.gpsimd
        def _(pool):
            def wide(a):
                return a.rearrange("p (q i) -> p q i", q=1).broadcast_to((128, GROUP, 128))

            def degdiag_step(g):
                pool.wait_ge(deg_ok, g + 1)
                pool.wait_ge(key_done, g)
                degree = deg[:, :].rearrange("p (q i) -> p q i", i=1).broadcast_to((128, GROUP, 128))
                nc.gpsimd.tensor_tensor(degdiag[:, :, :], wide(identb), degree, ALU.mult).then_inc(diag_ok, 1)

            def hsum_step(g, q):
                pool.wait_ge(hT_ok, g * SLOTS_PER_GROUP + q + 1)
                pool.wait_ge(base_ok, 2 * g + 2)
                nc.gpsimd.tensor_tensor(hsum[:, q, :], hT[:, q, :], base1[:, q, :], ALU.add).then_inc(hsum_ok, 1)

            def mlo_step(g, s, k):
                before = g * SLOTS_PER_GROUP + s
                pool.wait_ge(mmid_ok[k], before + 1)
                pool.wait_ge(mrest_ok[k], before + 1)
                nc.gpsimd.tensor_tensor(mparts[k][s % 2][:, 2, :, :], mrest[k][:, :, :], mparts[k][s % 2][:, 1, :, :],
                                        ALU.subtract).then_inc(mlo_ok[k], 1)

            def lo_step(g, s):
                k = g * SLOTS_PER_GROUP + s
                pool.wait_ge(uvmid_ok, k + 1)
                pool.wait_ge(uvrest_ok, k + 1)
                nc.gpsimd.tensor_tensor(parts[:, s, 2, :], uvrest[s % 2][:, :], parts[:, s, 1, :], ALU.subtract)\
                    .then_inc(uvlo_ok, 1)

            def group(g, first=False, last=False):
                for n in range(UNITS):
                    if n == 0: lo_step(g, 2)
                    if n == 1: mlo_step(g, 0, 0)
                    if n == 2 and not last: degdiag_step(g + 1)
                    if n == 2: mlo_step(g, 0, 1)
                    if n == 3: lo_step(g, 3)
                    if n == 4: mlo_step(g, 1, 0)
                    if n == 5: mlo_step(g, 1, 1)
                    if n == 6: hsum_step(g, 0)
                    if n == 6: lo_step(g, 4)
                    if n == 7: mlo_step(g, 2, 0)
                    if n == 8: mlo_step(g, 2, 1)
                    if n == 9: hsum_step(g, 1)
                    if n == 9: lo_step(g, 5)
                    if n == 10: mlo_step(g, 3, 0)
                    if n == 11: mlo_step(g, 3, 1)
                    if n == 12: hsum_step(g, 2)
                    if n == 12: lo_step(g, 6)
                    if n == 13: mlo_step(g, 4, 0)
                    if n == 14: mlo_step(g, 4, 1)
                    if n == 15: hsum_step(g, 3)
                    if n == 15: lo_step(g, 7)
                    if n == 16: mlo_step(g, 5, 0)
                    if n == 17: mlo_step(g, 5, 1)
                    if n == 18 and not last: lo_step(g + 1, 0)
                    if n == 19: mlo_step(g, 6, 0)
                    if n == 20: mlo_step(g, 6, 1)
                    if n == 21 and not last: lo_step(g + 1, 1)
                    if n == 22: mlo_step(g, 7, 0)
                    if n == 23: mlo_step(g, 7, 1)

            degdiag_step(0)
            for s in range(2):
                lo_step(0, s)
            group(0, first=True)
            with pool.Fori(1, GROUPS - 1) as g:
                group(g)
            group(GROUPS - 1, last=True)

        @block.vector
        def _(dve):
            V = nc.vector

            def wide(a):
                return a.rearrange("p (q i) -> p q i", q=1).broadcast_to((128, GROUP, 128))

            def col(a):
                return a[:, :].rearrange("p (q i) -> p q i", i=1).broadcast_to((128, GROUP, 128))

            def deg_step(g):
                dve.wait_ge(adj_loaded, 16 * (g + 1))
                dve.wait_ge(diag_ok, g)
                for q in range(GROUP):
                    last = V.tensor_scalar(junk[:, q, :], adj_in[:, q, :], 0.0, None, ALU.not_equal, ALU.add,
                                           accum_out=deg[:, q:q + 1])
                last.then_inc(deg_ok, 1)
                dve.wait_ge(deg_ok, g + 1)
                V.tensor_scalar(key[:, :], deg[:, :], tie, None, ALU.add).then_inc(key_ok, 1)

            def place_step(g):
                dve.wait_ge(key_done, g + 1)
                dve.wait_ge(key_ok, g + 1)
                V.tensor_tensor(above[:, :, :], PA[:, :, :], col(key), ALU.is_gt).then_inc(above_ok, 1)
                dve.wait_ge(above_ok, g + 1)
                V.tensor_reduce(place[:, :], above[:, :, :], AX.X, ALU.add).then_inc(place_ok, 1)

            def perm_step(g):
                dve.wait_ge(place_ok, g + 1)
                dve.wait_ge(permT_done, g)
                dve.wait_ge(xT_done, g)
                V.tensor_tensor(perm[:, :, :], wide(iota), col(place), ALU.is_equal).then_inc(perm_ok, 1)

            def adj_step(g):
                dve.wait_ge(adj2_ok, g + 1)
                dve.wait_ge(rank_done, g)
                V.tensor_scalar(nz[:, :, :], adj2[:, :, :], 0.0, None, ALU.not_equal).then_inc(nz_ok, 1)
                dve.wait_ge(adjhi_ok, g + 1)
                dve.wait_ge(adjmid_ok, g)
                V.tensor_tensor(adjrest[:, :, :], adj2[:, :, :], adjp[:, 0, :, :], ALU.subtract)\
                    .then_inc(adjrest_ok, 1)

            def adjlo_step(g):
                dve.wait_ge(adjmid_ok, g + 1)
                V.tensor_tensor(adjp[:, 2, :, :], adjrest[:, :, :], adjp[:, 1, :, :], ALU.subtract)\
                    .then_inc(adjlo_ok, 1)

            def rank_step(g):
                dve.wait_ge(rank_done, g + 1)
                V.tensor_tensor(rank[:, :, :], PB[:, :, :], nz[:, :, :], ALU.mult).then_inc(rank_ok, 1)
                V.scalar_tensor_tensor(out=junk[:, :, :], in0=PB[:, :, :], scalar=0.0, in1=wide(caps),
                                       op0=ALU.add, op1=ALU.is_gt, accum_out=over[:, bass.ds(g, 1)])\
                    .then_inc(over_ok, 1)

            def base_step(g, l):
                if l == 0:
                    dve.wait_ge(rowsum_ok, g + 1)
                    dve.wait_ge(xT_ok, g + 1)
                else:
                    dve.wait_ge(hsum_ok, g * GROUP)
                V.scalar_tensor_tensor(out=(base0, base1)[l][:, :, :], in0=rowsum[:, :, :], scalar=b2col[:, l:l + 1],
                                       in1=xT[:, :, :], op0=ALU.mult, op1=ALU.add).then_inc(base_ok, 1)

            def take_step(g, q):
                dve.wait_ge(rank_ok, g + 1)
                if not isinstance(g, int) or g:
                    dve.wait_ge(z_done, (g - 1) * UNITS + (GROUP + q + 1) * QUADS)
                r0 = off = 0
                for rows, cap in REGIONS:
                    n = rows * cap
                    o = take[:, q, off:off + n].rearrange("p (k i) -> p k i", i=rows)
                    c = rankc[:, off:off + n].rearrange("p (k i) -> p k i", i=rows)
                    r = rank[:, q, r0:r0 + rows].rearrange("p (k i) -> p k i", k=1).broadcast_to((128, cap, rows))
                    last = V.tensor_tensor(o, r, c, ALU.is_equal)
                    r0, off = r0 + rows, off + n
                last.then_inc(take_ok, 1)

            def W_step(g, q):
                dve.wait_ge(value_done, g * GROUP + q + 1)
                if not isinstance(g, int) or g:
                    dve.wait_ge(sum_done, (g - 1) * UNITS + (GROUP + q + 1) * QUADS)
                split, whole = [bank[:, :, :].rearrange("p q i -> p (q i)") for bank in (PA, PB)]
                V.tensor_tensor(Wparts[:, q, :], split[:, 0:SPLIT_W], mask[:, 0:SPLIT_W], ALU.mult)
                V.tensor_tensor(W[:, q, :], whole[:, 0:WHOLE_W], mask[:, SPLIT_W:SPLIT_W + WHOLE_W], ALU.mult)\
                    .then_inc(W_ok, 1)

            def mrest_step(g, s, k):
                before = g * SLOTS_PER_GROUP + s
                dve.wait_ge(mhi_ok[k], before + 1)
                dve.wait_ge(mlo_ok[k], before)
                dve.wait_ge(mmid_ok[k], before)
                V.scalar_tensor_tensor(out=mrest[k][:, :, :], in0=Z[k][:, :, :], scalar=0.0,
                                       in1=mparts[k][s % 2][:, 0, :, :], op0=ALU.max, op1=ALU.subtract)\
                    .then_inc(mrest_ok[k], 1)

            def sT_step(g, s):
                k = g * SLOTS_PER_GROUP + s
                dve.wait_ge(sum_done, QUADS * (k + 1))
                if s >= 2 or not isinstance(g, int) or g:
                    dve.wait_ge(msg_done, k - 1)
                V.tensor_reduce(sT[s % 2][:, 0:SPLIT_ROWS], PS[:, 0:3, 0:SPLIT_ROWS].rearrange("p v i -> p i v"),
                                AX.X, ALU.add)
                V.tensor_copy(sT[s % 2][:, SPLIT_ROWS:128], PS[:, 0, SPLIT_ROWS:128]).then_inc(sT_ok, 1)

            def b1_step():
                p = slice(96, 128)
                V.tensor_copy(b1parts[p, 0, :, :], b1row[p, :, :]).then_inc(b1_ok[0], 1)
                dve.wait_ge(b1_ok[0], 1)
                V.tensor_tensor(b1rest[p, :, :], b1row[p, :, :], b1parts[p, 0, :, :], ALU.subtract).then_inc(b1_ok[1], 1)
                dve.wait_ge(b1_ok[1], 1)
                V.tensor_copy(b1parts[p, 1, :, :], b1rest[p, :, :]).then_inc(b1_ok[2], 1)
                dve.wait_ge(b1_ok[2], 1)
                V.tensor_tensor(b1parts[p, 2, :, :], b1rest[p, :, :], b1parts[p, 1, :, :], ALU.subtract)\
                    .then_inc(b1_ok[3], 1)
                dve.wait_ge(b1_ok[3], 1)
                V.tensor_scalar(b1mix[0][p, :, :], b1parts[p, 0, :, :], ident[p, 96:97], None, ALU.mult)\
                    .then_inc(b1_ok[4], 1)
                for i in (1, 2):
                    dve.wait_ge(b1_ok[3 + i], 1)
                    V.scalar_tensor_tensor(out=b1mix[i][p, :, :], in0=b1parts[p, i, :, :], scalar=ident[p, 96 + i:97 + i],
                                           in1=b1mix[i - 1][p, :, :], op0=ALU.mult, op1=ALU.add).then_inc(b1_ok[4 + i], 1)
                dve.wait_ge(b1_ok[6], 1)
                for l in range(LAYERS):
                    o = ustack[p, GROUP * l:GROUP * l + GROUP, :, :].rearrange("p s b d -> p (s b) d")
                    V.tensor_copy(o, b1mix[2][p, l:l + 1, :].broadcast_to((32, GROUP * len(BLOCKS), D))).then_inc(b1_ok[6], 1)

            def rest_step(g, s):
                k = g * SLOTS_PER_GROUP + s
                dve.wait_ge(uvhi_ok, k + 1)
                if s >= 2 or not isinstance(g, int) or g:
                    dve.wait_ge(uvlo_ok, k - 1)
                V.tensor_tensor(uvrest[s % 2][:, :], PU[:, 0:2 * D], parts[:, s, 0, :], ALU.subtract)\
                    .then_inc(uvrest_ok, 1)

            def h_step(g, s):
                dve.wait_ge(msg_done, g * SLOTS_PER_GROUP + s + 1)
                q = s % GROUP
                if s < GROUP:
                    dve.wait_ge(base_ok, 2 * g + 1)
                    if q == 0:
                        dve.wait_ge(uv_done, g * SLOTS_PER_GROUP)
                        dve.wait_ge(hsum_ok, g * GROUP)
                    V.tensor_tensor(hT[:, q, :], PM[:, 0:128], base0[:, q, :], ALU.add).then_inc(hT_ok, 1)
                else:
                    dve.wait_ge(hsum_ok, g * GROUP + q + 1)
                    if q >= 2 or not isinstance(g, int) or g:
                        dve.wait_ge(yp_done, g * GROUP + q - 1)
                    V.tensor_tensor(yT[q % 2][:, :], PM[:, 0:128], hsum[:, q, :], ALU.add).then_inc(hT_ok, 1)

            def norm_stats(g):
                dve.wait_ge(y_ok, (g + 1) * GROUP)
                for q in range(GROUP):
                    last = V.bn_stats(stats[:, q, :], y[:, q, :])
                last.then_inc(stats_ok, 1)
                dve.wait_ge(stats_ok, g + 1)
                V.memset(varE[:, :], 0.0)
                for q in range(GROUP):
                    last = V.bn_aggr(meanvar[:, q, :], stats[:, q, :])
                last.then_inc(mv_ok, 1)
                dve.wait_ge(mv_ok, g + 1)
                V.tensor_scalar(varE[:, :], meanvar[:, :, 1], EPS, None, ALU.add).then_inc(varE_ok, 1)

            def rstd_step(n, k):
                V.reciprocal(inv[:, 0:n], root[:, 0:n]).then_inc(inv_ok, 1)
                dve.wait_ge(inv_ok, k + 1)
                V.tensor_tensor(quot[:, 0:n], varE[:, 0:n], inv[:, 0:n], ALU.mult).then_inc(quot_ok, 1)
                dve.wait_ge(quot_ok, k + 1)
                V.tensor_tensor(twice[:, 0:n], quot[:, 0:n], root[:, 0:n], ALU.add).then_inc(twice_ok, 1)
                dve.wait_ge(twice_ok, k + 1)
                V.tensor_scalar(half[:, 0:n], twice[:, 0:n], 0.5, None, ALU.mult).then_inc(half_ok, 1)
                dve.wait_ge(half_ok, k + 1)
                V.reciprocal(rstd[:, 0:n], half[:, 0:n]).then_inc(rstd_ok, 1)
                dve.wait_ge(rstd_ok, k + 1)

            def norm_rstd(g):
                dve.wait_ge(root_ok, g + 1)
                rstd_step(GROUP, g)

            def norm_out(g):
                dve.wait_ge(outs_free, 16 * (g + 1))
                for q in range(GROUP):
                    last = V.tensor_scalar(outs[:, q, :], y[:, q, :], meanvar[:, q, 0:1], rstd[:, q:q + 1],
                                           ALU.subtract, ALU.mult)
                last.then_inc(outs_ok, 1)

            def group(g, first=False, last=False):
                for n in range(UNITS):
                    if n == 1 and not first: sT_step(g - 1, 7)
                    if n % QUADS == 1 and n > 1: sT_step(g, n // QUADS - 1)
                    if n % QUADS < SPLIT_QUADS: mrest_step(g, n // QUADS, n % QUADS)
                    if n == 0: rest_step(g, 2)
                    if n == 0: W_step(g, 1)
                    if n == 1 and not last: deg_step(g + 1)
                    if n == 2 and not first: h_step(g - 1, 7)
                    if n == 2: take_step(g, 3)
                    if n == 3: rest_step(g, 3)
                    if n == 3: W_step(g, 2)
                    if n == 5: h_step(g, 0)
                    if n == 5 and not last: place_step(g + 1)
                    if n == 6: rest_step(g, 4)
                    if n == 6 and not last: perm_step(g + 1)
                    if n == 6: W_step(g, 3)
                    if n == 8: h_step(g, 1)
                    if n == 8 and not first: norm_stats(g - 1)
                    if n == 9: rest_step(g, 5)
                    if n == 10 and not first: norm_rstd(g - 1)
                    if n == 11: h_step(g, 2)
                    if n == 11 and not first: norm_out(g - 1)
                    if n == 12: rest_step(g, 6)
                    if n == 12 and not last: adj_step(g + 1)
                    if n == 14: h_step(g, 3)
                    if n == 14 and not last: rank_step(g + 1)
                    if n == 15: rest_step(g, 7)
                    if n == 15 and not last: adjlo_step(g + 1)
                    if n == 17: h_step(g, 4)
                    if n == 17 and not last: take_step(g + 1, 0)
                    if n == 18 and not last: rest_step(g + 1, 0)
                    if n == 19 and not last: base_step(g + 1, 0)
                    if n == 20: h_step(g, 5)
                    if n == 20 and not last: take_step(g + 1, 1)
                    if n == 21 and not last: rest_step(g + 1, 1)
                    if n == 21 and not last: W_step(g + 1, 0)
                    if n == 22 and not last: base_step(g + 1, 1)
                    if n == 23: h_step(g, 6)
                    if n == 23 and not last: take_step(g + 1, 2)
                    if n == 6 and last:
                        dve.wait_ge(over_ok, GROUPS)
                        V.tensor_reduce(overs[:, :], over[:, :], AX.X, ALU.add).then_inc(overs_ok, 1)
                        dve.wait_ge(overs_ok, 1)
                        V.tensor_scalar(some[:, :], overs[:, :], 1.0, None, ALU.min).then_inc(some_ok, 1)
                    if n == 9 and last:
                        dve.wait_ge(count_done, 1)
                        V.tensor_copy(flag[:, :], PA[:, 0, 0:1]).then_inc(flag_ok, 1)

            V.memset(outs[:, :, :], 0.0).then_inc(outs_free, 16)
            dve.wait_ge(const_in, 32)
            deg_step(0)
            place_step(0)
            perm_step(0)
            dve.wait_ge(w_in, 64)
            b1_step()
            adj_step(0)
            rest_step(0, 0)
            adjlo_step(0)
            rank_step(0)
            rest_step(0, 1)
            dve.wait_ge(tables_in, 32)
            take_step(0, 0)
            take_step(0, 1)
            W_step(0, 0)
            take_step(0, 2)
            for l in range(LAYERS):
                base_step(0, l)
            group(0, first=True)
            with dve.Fori(1, GROUPS - 1) as g:
                group(g)
            group(GROUPS - 1, last=True)
            g = GROUPS - 1
            sT_step(g, 7)
            h_step(g, 7)
            norm_stats(g)
            norm_rstd(g)
            norm_out(g)

            def general(b):
                for l in range(LAYERS):
                    dve.wait_ge(g_uv, 2 * b + l + 1)
                    V.tensor_tensor(uvg[:, 0:D], PU[:, 0:D], b1row[:, l, :], ALU.add)
                    V.tensor_copy(uvg[:, D:2 * D], PU[:, D:2 * D]).then_inc(g_uv_ok, 1)
                    with dve.Fori(0, STEPS) as i:
                        dve.wait_ge(g_uv_ok, 2 * b + l + 1)
                        n = (b * LAYERS + l) * STEPS + i + 1
                        u = uvg[:, 0:D].rearrange("p (r d) -> p r d", r=1).broadcast_to((128, 4, D))
                        pickrow = ident[:, bass.ds(4 * i, 4)].rearrange("p (r d) -> p r d", d=1).broadcast_to((128, 4, D))
                        V.tensor_tensor(spread[:, :, :], u, pickrow, ALU.mult).then_inc(g_spread_ok, 1)
                        dve.wait_ge(g_rows, n)
                        v = uvg[:, D:2 * D].rearrange("p (r d) -> p r d", r=1).broadcast_to((128, 4, D))
                        V.tensor_tensor(pairs[:, :, :], Z[0][:, :, :], v, ALU.add).then_inc(g_pairs_ok, 1)
                    h = (xT, hT)[l]
                    V.scalar_tensor_tensor(out=baseg[:, :], in0=rowsum[:, 0, :], scalar=b2col[:, l:l + 1],
                                           in1=h[:, 0, :], op0=ALU.mult, op1=ALU.add).then_inc(g_base_ok, 1)
                    dve.wait_ge(g_base_ok, 3 * b + l + 1)
                    if l == 1:
                        V.tensor_tensor(baseg[:, :], baseg[:, :], xT[:, 0, :], ALU.add).then_inc(g_base_ok, 1)
                        dve.wait_ge(g_base_ok, 3 * b + 3)
                    dve.wait_ge(g_msg, 2 * b + l + 1)
                    V.tensor_tensor(hT[:, 0, :], PM[:, 0:128], baseg[:, :], ALU.add).then_inc(g_h_ok, 1)
                dve.wait_ge(g_y_ok, b + 1)
                V.bn_stats(stats[:, 0, :], y[:, 0, :]).then_inc(g_stats_ok, 1)
                dve.wait_ge(g_stats_ok, b + 1)
                V.memset(varE[:, :], 0.0)
                V.bn_aggr(meanvar[:, 0, :], stats[:, 0, :]).then_inc(g_mv_ok, 1)
                dve.wait_ge(g_mv_ok, b + 1)
                V.tensor_scalar(varE[:, 0:1], meanvar[:, 0, 1:2], EPS, None, ALU.add).then_inc(g_var_ok, 1)
                dve.wait_ge(g_root_ok, b + 1)
                rstd_step(1, GROUPS + b)
                dve.wait_ge(g_stored, 16 * (b + 1))
                V.tensor_scalar(outs[:, 0, :], y[:, 0, :], meanvar[:, 0, 0:1], rstd[:, 0:1],
                                ALU.subtract, ALU.mult).then_inc(g_out_ok, 1)

            with dve.If(overflow(dve) > 0):
                dve.wait_ge(outs_free, 16 * (GROUPS + 1))
                V.memset(onesf[:, :], 1.0).then_inc(onesf_ok, 1)
                V.memset(outs[:, 0, :], 0.0).then_inc(g_stored, 16)
                with dve.Fori(0, GRAPHS) as b:
                    general(b)


_INS = ['x', 'adj', 'L0_gnn_w1', 'L0_gnn_b1', 'L0_gnn_w2', 'L0_gnn_b2']


def kernel(**inputs):
    import numpy as _np
    import concourse.bacc as _bacc
    from concourse import mybir as _mybir
    from concourse.bass_utils import run_bass_kernel_spmd as _run

    nc = _bacc.Bacc("TRN2", target_bir_lowering=False, num_devices=1)
    cf, cb = constants()
    arrays, args = {}, []
    for name, a in [(n, inputs[n]) for n in _INS] + [('tables_f32', cf), ('tables_bf16', cb)]:
        a = _np.ascontiguousarray(a)
        arrays[f"in_{name}_dram"] = a
        args.append(nc.dram_tensor(f"in_{name}_dram", a.shape, _mybir.dt.from_np(a.dtype), kind="ExternalInput").ap())
    out = nc.dram_tensor("out_0_dram", (GRAPHS, NODES, D), _mybir.dt.float32, kind="ExternalOutput").ap()
    gnn_kernel(nc, *args, out)
    r = _run(nc, [arrays], core_ids=[0])
    return r.results[0]["out_0_dram"]
```
